# Optimizing a Trainium2 kernel written in Bass

```python
import numpy as np
import jax
import jax.numpy as jnp

def _softmax(x, axis=-1):
    return jax.nn.softmax(x, axis=axis)

def _gelu(x):
    return jax.nn.gelu(x, approximate=True)

def _silu(x):
    return jax.nn.silu(x)

def _sigmoid(x):
    return jax.nn.sigmoid(x)

def _layernorm(x, axis=-1, eps=1e-05):
    m = jnp.mean(x, axis=axis, keepdims=True)
    v = jnp.var(x, axis=axis, keepdims=True)
    return (x - m) / jnp.sqrt(v + eps)

def _scatter_add(tgt, idx, src, axis=0):
    return tgt.at[idx].add(src)

def _segment_sum(src, seg, n):
    return jax.ops.segment_sum(src, seg, n)
kernel_name = 'mk_macaron_d1_jaxref_r8_aeff4c'

def setup_inputs(seed: int=0):
    np.random.seed(seed)
    _w = jnp.asarray

    def _L0_attn_setup():
        import jax, jax.numpy as jnp
        import numpy as np
        B, S, D, H = (2, 256, 128, 16)
        HD = D // H

        def alibi_slopes(num_heads):
            x = (2.0 ** 8) ** (1.0 / num_heads)
            return jnp.array([1.0 / x ** (i + 1) for i in range(num_heads)], dtype=jnp.float32)
        key = jax.random.key(seed)
        ks = jax.random.split(key, 5)
        scale = 1.0 / np.sqrt(D)
        return {'x': jax.random.normal(ks[0], (B, S, D), dtype=jnp.float32), 'Wq': jax.random.normal(ks[1], (D, D), dtype=jnp.float32) * scale, 'Wk': jax.random.normal(ks[2], (D, D), dtype=jnp.float32) * scale, 'Wv': jax.random.normal(ks[3], (D, D), dtype=jnp.float32) * scale, 'Wo': jax.random.normal(ks[4], (D, D), dtype=jnp.float32) * scale}
    _L0_attn_in = _L0_attn_setup()

    def _L0_ffn_setup():
        import jax, jax.numpy as jnp
        import numpy as np
        D = 128
        F = 128
        E = 8
        K = 2
        B, T = (2, 256)

        def _moe_forward(x, router_w, w1, w2, shared_gate_up, shared_down, shared_gate_w):
            b, t, d = x.shape
            xf = x.reshape(-1, d)
            n = xf.shape[0]
            logits = xf @ router_w
            probs = jax.nn.softmax(logits, axis=-1)
            topw, topi = jax.lax.top_k(probs, K)
            combine = jnp.zeros((n, E), dtype=probs.dtype).at[jnp.arange(n)[:, None], topi].add(topw)
            h = jax.nn.silu(jnp.einsum('nd,edf->nef', xf, w1))
            ye = jnp.einsum('nef,efd->ned', h, w2)
            routed = jnp.einsum('ne,ned->nd', combine, ye)
            gu = xf @ shared_gate_up
            gate, up = (gu[:, :F], gu[:, F:])
            shared = jax.nn.silu(gate) * up @ shared_down
            shared = jax.nn.sigmoid(xf @ shared_gate_w) * shared
            return (routed + shared).reshape(b, t, d)
        key = jax.random.key(seed)
        ks = jax.random.split(key, 7)
        std = 0.02
        x = jax.random.normal(ks[0], (B, T, D), dtype=jnp.float32)
        router_w = jax.random.normal(ks[1], (D, E), dtype=jnp.float32) * std
        w1 = jax.random.normal(ks[2], (E, D, F), dtype=jnp.float32) * std
        w2 = jax.random.normal(ks[3], (E, F, D), dtype=jnp.float32) * std
        shared_gate_up = jax.random.normal(ks[4], (D, 2 * F), dtype=jnp.float32) * std
        shared_down = jax.random.normal(ks[5], (F, D), dtype=jnp.float32) * std
        shared_gate_w = jax.random.normal(ks[6], (D, 1), dtype=jnp.float32) * std
        return {'x': x, 'router_w': router_w, 'w1': w1, 'w2': w2, 'shared_gate_up': shared_gate_up, 'shared_down': shared_down, 'shared_gate_w': shared_gate_w}
    _L0_ffn_in = _L0_ffn_setup()
    _d = {'L0_attn_x': _L0_attn_in['x'], 'L0_attn_Wq': _L0_attn_in['Wq'], 'L0_attn_Wk': _L0_attn_in['Wk'], 'L0_attn_Wv': _L0_attn_in['Wv'], 'L0_attn_Wo': _L0_attn_in['Wo'], 'L0_ffn_router_w': _L0_ffn_in['router_w'], 'L0_ffn_w1': _L0_ffn_in['w1'], 'L0_ffn_w2': _L0_ffn_in['w2'], 'L0_ffn_shared_gate_up': _L0_ffn_in['shared_gate_up'], 'L0_ffn_shared_down': _L0_ffn_in['shared_down'], 'L0_ffn_shared_gate_w': _L0_ffn_in['shared_gate_w']}
    _x0 = _d['L0_attn_x']
    _d['L0_attn_x'] = jax.random.normal(jax.random.fold_in(jax.random.key(seed), 1), (4, 512, 128), dtype=_x0.dtype)
    del _x0
    return _d

def reference(L0_attn_x, L0_attn_Wq, L0_attn_Wk, L0_attn_Wv, L0_attn_Wo, L0_ffn_router_w, L0_ffn_w1, L0_ffn_w2, L0_ffn_shared_gate_up, L0_ffn_shared_down, L0_ffn_shared_gate_w):

    def _L0_attn_ref(x, Wq, Wk, Wv, Wo):
        import jax, jax.numpy as jnp
        import numpy as np
        B, S, D, H = (2, 256, 128, 16)
        HD = D // H

        def alibi_slopes(num_heads):
            x = (2.0 ** 8) ** (1.0 / num_heads)
            return jnp.array([1.0 / x ** (i + 1) for i in range(num_heads)], dtype=jnp.float32)
        b, s, d = x.shape
        q = (x @ Wq.T).reshape(b, s, H, HD).transpose(0, 2, 1, 3)
        k = (x @ Wk.T).reshape(b, s, H, HD).transpose(0, 2, 1, 3)
        v = (x @ Wv.T).reshape(b, s, H, HD).transpose(0, 2, 1, 3)
        scores = jnp.einsum('bhqd,bhkd->bhqk', q, k) / jnp.sqrt(jnp.float32(HD))
        rel = (jnp.arange(s)[None, :] - jnp.arange(s)[:, None]).astype(jnp.float32)
        m = alibi_slopes(H)[:, None, None]
        scores = scores - (m * rel)[None]
        causal_mask = jnp.tril(jnp.ones((s, s), dtype=bool))
        scores = jnp.where(causal_mask[None, None], scores, -jnp.inf)
        attn = jax.nn.softmax(scores, axis=-1)
        out = jnp.einsum('bhqk,bhkd->bhqd', attn, v)
        out = out.transpose(0, 2, 1, 3).reshape(b, s, d)
        return out @ Wo.T

    def _L0_ffn_ref(x, router_w, w1, w2, shared_gate_up, shared_down, shared_gate_w):
        import jax, jax.numpy as jnp
        import numpy as np
        D = 128
        F = 128
        E = 8
        K = 2
        B, T = (2, 256)

        def _moe_forward(x, router_w, w1, w2, shared_gate_up, shared_down, shared_gate_w):
            b, t, d = x.shape
            xf = x.reshape(-1, d)
            n = xf.shape[0]
            logits = xf @ router_w
            probs = jax.nn.softmax(logits, axis=-1)
            topw, topi = jax.lax.top_k(probs, K)
            combine = jnp.zeros((n, E), dtype=probs.dtype).at[jnp.arange(n)[:, None], topi].add(topw)
            h = jax.nn.silu(jnp.einsum('nd,edf->nef', xf, w1))
            ye = jnp.einsum('nef,efd->ned', h, w2)
            routed = jnp.einsum('ne,ned->nd', combine, ye)
            gu = xf @ shared_gate_up
            gate, up = (gu[:, :F], gu[:, F:])
            shared = jax.nn.silu(gate) * up @ shared_down
            shared = jax.nn.sigmoid(xf @ shared_gate_w) * shared
            return (routed + shared).reshape(b, t, d)
        return _moe_forward(x, router_w, w1, w2, shared_gate_up, shared_down, shared_gate_w)
    x = L0_attn_x
    x = x + 0.5 * _L0_ffn_ref(_layernorm(x, axis=-1), L0_ffn_router_w, L0_ffn_w1, L0_ffn_w2, L0_ffn_shared_gate_up, L0_ffn_shared_down, L0_ffn_shared_gate_w)
    x = x + _L0_attn_ref(_layernorm(x, axis=-1), L0_attn_Wq, L0_attn_Wk, L0_attn_Wv, L0_attn_Wo)
    x = x + 0.5 * _L0_ffn_ref(_layernorm(x, axis=-1), L0_ffn_router_w, L0_ffn_w1, L0_ffn_w2, L0_ffn_shared_gate_up, L0_ffn_shared_down, L0_ffn_shared_gate_w)
    return x

_drawn_inputs = setup_inputs


def setup_inputs(seed=0):
    import zlib

    import numpy as np

    out = dict(_drawn_inputs(seed))
    spreads = {}
    factors = {'L0_ffn_router_w': 8.0,
     'L0_ffn_w1': 8.0,
     'L0_ffn_w2': 8.0,
     'L0_ffn_shared_gate_up': 8.0,
     'L0_ffn_shared_down': 8.0,
     'L0_ffn_shared_gate_w': 8.0}
    for name, (base, spread) in spreads.items():
        noise = np.random.default_rng([zlib.crc32(name.encode()), seed]).standard_normal(out[name].shape)
        drawn = base * np.exp(spread * noise) if base else spread * noise
        out[name] = jnp.asarray(drawn.astype(out[name].dtype))
    for name, factor in factors.items():
        out[name] = (out[name] * factor).astype(out[name].dtype)
    return out
```

```python
import concourse.bass as bass
from concourse import mybir
from contextlib import ExitStack


def macaron_block(nc: bass.Bass, x, w1, w2, gate_up, down, router, wq, wk, wv, wo,
                  q_const, k_const, select, earlier, causal, ident, ident_b, out):
    f32, f32r, bf16 = mybir.dt.float32, mybir.dt.float32r, mybir.dt.bfloat16
    i32 = mybir.dt.int32
    ALU, ACT, AX = mybir.AluOpType, mybir.ActivationFunctionType, mybir.AxisListType

    P = 128
    B, S, D = x.shape
    E, _, F = w1.shape
    NT = S // P
    H, HD = 16, D // 16
    NP = H // 2
    GH = 4
    NG = H // GH
    C = E + 1
    PARTS = 3
    PROD = 6 * HD
    ROWS_S, ROWS_T = PROD + 6, PROD + 9
    VW = 32
    EPS = 1e-5
    RSQRT_MAGIC = float(0x5F3759DF)
    SPAN = 1280
    WID = [S - P * kt for kt in range(NT)]

    ctx = ExitStack()
    with ctx:
        def sb(name, shape, dt=f32):
            return ctx.enter_context(nc.sbuf_tensor(name, shape, dt))

        def sem(name):
            return ctx.enter_context(nc.semaphore(name))

        NW = E * F + 2 * F + 3 * D
        w_raw = sb("w_raw", [P, NW])
        w_hi, w_lo = sb("w_hi", [P, NW], f32r), sb("w_lo", [P, NW], f32r)
        rt_raw, rt_hi, rt_lo = sb("rt_raw", [P, 10]), sb("rt_hi", [P, 10], f32r), sb("rt_lo", [P, 10], f32r)
        w2_sb = sb("w2_sb", [P, C, D])
        wo_sb = sb("wo_sb", [P, D])
        id_f, id_b = sb("id_f", [P, P]), sb("id_b", [P, P], bf16)
        sel_sb = sb("sel_sb", [PARTS * C, C, P], bf16)
        earlier_sb = sb("earlier_sb", [P, E, E])
        causal_sb = sb("causal_sb", [P, P], bf16)
        X = sb("X", [P, B * NT, D])
        stats, mv, rstd = sb("stats", [P, NT, 6]), sb("mv", [P, NT, 2]), sb("rstd", [P, NT])
        vhalf, newton = sb("vhalf", [P, NT]), sb("newton", [P, NT])
        XN = sb("XN", [P, NT, D])
        XH, XL = sb("XH", [P, 2, S], f32r), sb("XL", [P, 2, S], f32r)
        nmx, shifted, ex = sb("nmx", [P, NT]), sb("shifted", [P, NT, E]), sb("ex", [P, NT, E])
        th, ssum, rsum = sb("th", [P, NT]), sb("ssum", [P, NT]), sb("rsum", [P, NT])
        above, level = sb("above", [P, NT, E, E]), sb("level", [P, NT, E, E])
        rank, kept, coef = sb("rank", [P, NT, E]), sb("kept", [P, NT, E]), sb("coef", [P, NT, C])
        rest = sb("rest", [P, NT, C])
        coef3 = sb("coef3", [P, NT, PARTS, C], bf16)
        coefT = sb("coefT", [PARTS * C, 2, S], bf16)
        act = sb("act", [P, 3, S])
        gated = sb("gated", [P, S])
        hid = sb("hid", [P, 3, S])
        YT = sb("YT", [P, S])
        qk_f, qk_rest = sb("qk_f", [P, 2, S]), sb("qk_rest", [P, 2, S])
        qk_parts = sb("qk_parts", [P, 2, PARTS, S], bf16)
        QA = [sb(f"QA{i}", [P, NP, S], bf16) for i in range(2)]
        KA = [sb(f"KA{i}", [P, NP, S], bf16) for i in range(2)]
        VA = [sb(f"VA{i}", [P, NT, H, VW]) for i in range(2)]
        nmax = sb("nmax", [P, 2, GH, NT])
        nmax_rest = sb("nmax_rest", [P, GH, NT])
        nmax3 = sb("nmax3", [P, NT, GH, PARTS], bf16)
        nmaxT = sb("nmaxT", [GH * PARTS, 2, S], bf16)
        probs = [sb(f"probs{i}", [P, GH, SPAN]) for i in range(2)]
        OT = sb("OT", [P, S])
        rden = sb("rden", [P, NT, GH])
        AO = sb("AO", [P, NT, D])
        AT = sb("AT", [P, S])
        scratch = nc.dram_tensor("qk_scratch", [2, B, P, 6, S], bf16, kind="Internal").ap()

        banks = [ctx.enter_context(nc.psum_tensor(f"bank{i}", [P, S], f32)) for i in range(8)]
        H_BANK, C_BANK, Y_BANK, M0, M1 = banks[0:3], banks[3:5], banks[5], banks[6], banks[7]
        S_BANK, T_BANK, O_BANK = banks[0:2], banks[2:5], banks[5]

        ld_x = [sem(f"ld_x{b}") for b in range(B)]
        ld_w, ld_wa, ld_c, ld_w2, ld_ac = sem("ld_w"), sem("ld_wa"), sem("ld_c"), sem("ld_w2"), sem("ld_ac")
        w_split = sem("w_split")
        va_set = sem("va_set")
        xn_ready, xt_ready, xh_ready, xl_ready = sem("xn_ready"), sem("xt_ready"), sem("xh_ready"), sem("xl_ready")
        lg_ready, shift_ready, ex_ready = sem("lg_ready"), sem("shift_ready"), sem("ex_ready")
        c3_ready, ct_ready, ct_sb = sem("c3_ready"), sem("ct_ready"), sem("ct_sb")
        h_ready, act_ready, c_ready, hid_ready = sem("h_ready"), sem("act_ready"), sem("c_ready"), sem("hid_ready")
        y_step, yt_sb, ytt_ready, x_ffn = sem("y_step"), sem("yt_sb"), sem("ytt_ready"), sem("x_ffn")
        up_used = sem("up_used")
        qk_ready, qk_sb, parts_ready = sem("qk_ready"), sem("qk_sb"), sem("parts_ready")
        v_ready, v_sb = sem("v_ready"), sem("v_sb")
        scr_q, scr_k = sem("scr_q"), sem("scr_k")
        qa_ready, ka_ready = [sem("qa_ready0"), sem("qa_ready1")], [sem("ka_ready0"), sem("ka_ready1")]
        ao_ready, aot_ready, at_sb, wo_ready, x_att = sem("ao_ready"), sem("aot_ready"), sem("at_sb"), sem("wo_ready"), sem("x_att")
        s_ready, s_used = sem("s_ready"), sem("s_used")
        nm3_ready, nmt_ready, nmt_sb = sem("nm3_ready"), sem("nmt_ready"), sem("nmt_sb")
        nm_rows = [sem("nm_rows0"), sem("nm_rows1")]
        t_ready, exp_done, masked = sem("t_ready"), sem("exp_done"), sem("masked")
        pv_ready, ot_sb, ott_ready, ott_used = sem("pv_ready"), sem("ot_sb"), sem("ott_ready"), sem("ott_used")
        stored = sem("stored")
        dve_chain, act_chain, pool_chain = sem("dve_chain"), sem("act_chain"), sem("pool_chain")

        block = ctx.enter_context(nc.Block())

        NJ = 2 * B
        HID = E + 2
        NU = 10

        def ln_index(kind, b):
            return kind * B + b

        def score_units(g):
            heads = range(GH * g, GH * g + GH)
            return ([[(0, h, 3)] for h in heads] + [[(0, h, 2), (3 * P, h, 0)] for h in heads]
                    + [[(0, h, 1), (2 * P, h + 2, 1)] for h in heads[:2]])

        def prob_units(g):
            heads = range(GH * g, GH * g + GH)
            return ([[(0, h, 0)] for h in heads] + [[(0, h, 3), (P, h, 1)] for h in heads]
                    + [[(0, h, 2), (2 * P, h + 2, 2)] for h in heads[:2]])

        POS = {0: 0, 3: 512, 1: 640, 2: 1024}

        @block.sync
        def _(sp):
            sp.dma_start(X[:, 0:NT, :], x[0].rearrange("(t p) d -> p t d", p=P)).then_inc(ld_x[0], 16)
            sp.dma_start(id_f[:, :], ident).then_inc(ld_c, 16)
            sp.dma_start(rt_raw[:, :], router).then_inc(ld_w, 16)
            for e in range(E):
                sp.dma_start(w_raw[:, e * F:(e + 1) * F], w1[e]).then_inc(ld_w, 16)
            sp.dma_start(w_raw[:, E * F:(E + 2) * F], gate_up).then_inc(ld_w, 16)
            sp.dma_start(id_b[:, :], ident_b).then_inc(ld_c, 16)
            sp.dma_start(sel_sb[:, :, :], select).then_inc(ld_c, 16)
            sp.dma_start(earlier_sb[:, :, :], earlier.partition_broadcast(P)).then_inc(ld_c, 16)
            sp.dma_start(w2_sb[:, 0:E, :], w2.rearrange("e f d -> f e d")).then_inc(ld_w2, 16)
            sp.dma_start(w2_sb[:, E, :], down).then_inc(ld_w2, 16)
            for b in range(1, B):
                sp.dma_start(X[:, b * NT:(b + 1) * NT, :], x[b].rearrange("(t p) d -> p t d", p=P)).then_inc(ld_x[b], 16)
            for i, w in enumerate((wq, wk, wv)):
                sp.dma_start(w_raw[:, (E + 2) * F + i * D:(E + 2) * F + (i + 1) * D], w).then_inc(ld_wa, 16)
            sp.dma_start(wo_sb[:, :], wo).then_inc(ld_ac, 16)
            sp.dma_start(causal_sb[:, :], causal).then_inc(ld_ac, 16)
            for i in range(2):
                for par in range(2):
                    sp.dma_start(QA[i][64 * par + PROD:64 * par + PROD + 6, :, :], q_const[par]).then_inc(ld_ac, 16)
                    sp.dma_start(KA[i][64 * par + PROD:64 * par + PROD + 9, :, :], k_const[par]).then_inc(ld_ac, 16)

            def scatter_rows(b):
                for i, (scr, to, ready) in enumerate(((scr_q, QA, qa_ready), (scr_k, KA, ka_ready))):
                    part = qk_parts[:, i]
                    sp.wait_ge(parts_ready, 2 * b + i + 1)
                    dst = scratch[i, b]
                    if i == 0:
                        sp.dma_start(dst[:, 0:3, :], part[:, 0, :].unsqueeze(1).broadcast_to([P, 3, S])).then_inc(scr, 16)
                        sp.dma_start(dst[:, 3:5, :], part[:, 1, :].unsqueeze(1).broadcast_to([P, 2, S])).then_inc(scr, 16)
                        sp.dma_start(dst[:, 5, :], part[:, 2, :]).then_inc(scr, 16)
                    else:
                        sp.dma_start(dst[:, 0:3, :], part[:, 0:3, :]).then_inc(scr, 16)
                        sp.dma_start(dst[:, 3:5, :], part[:, 0:2, :]).then_inc(scr, 16)
                        sp.dma_start(dst[:, 5, :], part[:, 0, :]).then_inc(scr, 16)
                for i, (scr, to, ready) in enumerate(((scr_q, QA, qa_ready), (scr_k, KA, ka_ready))):
                    if b >= 2:
                        sp.wait_ge(t_ready, NU * NG * (b - 1))
                    sp.wait_ge(scr, 48 * (b + 1))
                    rows = scratch[i, b].rearrange("(pair par d) s n -> par d s pair n", par=2, d=HD)
                    for par in range(2):
                        sp.dma_start(to[b % 2][64 * par:64 * par + PROD, :, :],
                                     rows[par].rearrange("d s pair n -> (d s) pair n")).then_inc(ready[b % 2], 16)

            def maximum_rows(G):
                b, g = divmod(G, NG)
                sp.wait_ge(nmt_sb, G + 1)
                for hh in range(GH):
                    h = GH * g + hh
                    sp.dma_start(QA[b % 2][64 * (h % 2) + ROWS_S:64 * (h % 2) + ROWS_T, h // 2, :],
                                 nmaxT[PARTS * hh:PARTS * (hh + 1), G % 2, :]).then_inc(nm_rows[G % 2], 16)

            scatter_rows(0)
            scatter_rows(1)
            for n in range(-1, B * NG - 1):
                maximum_rows(n + 1)
                if n > 0 and n % NG == 0 and n // NG + 1 < B:
                    scatter_rows(n // NG + 1)
            for b in range(B):
                sp.wait_ge(x_ffn, B + b + 1)
                sp.dma_start(out[b].rearrange("(t p) d -> p t d", p=P), X[:, b * NT:(b + 1) * NT, :]).then_inc(stored, 16)
            sp.wait_ge(stored, 16 * B)

        @block.gpsimd
        def _(pool):
            for i in range(2):
                nc.gpsimd.memset(VA[i][:, :, :, :], 0.0).then_inc(pool_chain, 1)
            pool.wait_ge(pool_chain, 2)
            for i in range(2):
                nc.gpsimd.memset(VA[i][:, :, :, HD:HD + 1], 1.0).then_inc(va_set, 1)
            for G in range(B * NG):
                for kt in (0, 3, 1, 2):
                    need = {0: 4, 3: 8, 1: 8, 2: 10}[kt]
                    pool.wait_ge(exp_done, NU * G + need)
                    blk = probs[G % 2][:, :, POS[kt]:POS[kt] + P]
                    nc.gpsimd.affine_select(out=blk, in_=blk, compare_op=ALU.is_ge, fill=0.0, base=0,
                                            pattern=[[0, GH], [1, P]], channel_multiplier=-1).then_inc(masked, 1)

        @block.scalar
        def _(ac):
            def split_xt(n):
                ac.wait_ge(xt_ready, n + 1)
                nc.scalar.activation(XH[:, n % 2, :], M0[:, :], ACT.Copy).then_inc(xh_ready, 1)

            def silu(i):
                j, n = divmod(i, C)
                ac.wait_ge(h_ready, HID * j + n + 1)
                if i >= 3:
                    ac.wait_ge(hid_ready, i - 2)
                nc.scalar.activation(act[:, i % 3, :], H_BANK[(HID * j + n) % 3][:, :], ACT.Silu).then_inc(act_ready, 1)

            def router_exp(j):
                ac.wait_ge(shift_ready, j + 1)
                nc.scalar.activation(th[:, :], M0[:, 0:10 * NT].rearrange("p (t e) -> p t e", e=10)[:, :, E],
                                     ACT.Tanh, scale=0.5).then_inc(ex_ready, 1)
                nc.scalar.activation(ex[:, :, :], shifted[:, :, :], ACT.Exp).then_inc(ex_ready, 1)

            def copy_y(j):
                ac.wait_ge(y_step, C * (j + 1))
                if j >= 1:
                    ac.wait_ge(ytt_ready, j)
                nc.scalar.activation(YT[:, :], Y_BANK[:, :], ACT.Copy).then_inc(yt_sb, 1)

            def ffn(kind):
                split_xt(ln_index(2 * kind, 0))
                router_exp(B * kind)
                for b in range(B):
                    j = B * kind + b
                    for n in range(C):
                        silu(C * j + n)
                        if n == 3 and b + 1 < B:
                            split_xt(ln_index(2 * kind, b + 1))
                        if n == 6 and b + 1 < B:
                            router_exp(j + 1)
                    copy_y(j)

            def copy_qk(b, i):
                ac.wait_ge(qk_ready, 2 * b + i + 1)
                if b >= 1:
                    ac.wait_ge(parts_ready, 2 * (b - 1) + i + 1)
                nc.scalar.activation(qk_f[:, i, :], M0[:, :], ACT.Copy,
                                     scale=float(HD) ** -0.5 if i == 0 else 1.0).then_inc(qk_sb, 1)

            def values(b):
                ac.wait_ge(v_ready, b + 1)
                ac.wait_ge(va_set, 2)
                if b >= 2:
                    ac.wait_ge(pv_ready, NG * (b - 1))
                nc.scalar.activation(VA[b % 2][:, :, :, 0:HD],
                                     M0[:, :].rearrange("p (t h d) -> p t h d", t=NT, d=HD), ACT.Copy).then_inc(v_sb, 1)

            def exps(G, i):
                u = NU * G + i
                ac.wait_ge(t_ready, u + 1)
                if i == 0 and G >= 2:
                    ac.wait_ge(pv_ready, G - 1)
                a = prob_units(G % NG)[i]
                head = a[0][1] - GH * (G % NG)
                bank = T_BANK[u % 3]
                if a[0][2] == 2:
                    dst = probs[G % 2][:, head:head + 3:2, POS[2]:POS[2] + 2 * P]
                    src = bank[:, :].rearrange("p (h n) -> p h n", h=2)
                else:
                    pos = POS[a[0][2]]
                    dst, src = probs[G % 2][:, head, pos:pos + S], bank[:, :]
                nc.scalar.activation(dst, src, ACT.Exp).then_inc(exp_done, 1)

            def copy_nmax(G):
                ac.wait_ge(nmt_ready, G + 1)
                if G >= 2:
                    ac.wait_ge(nm_rows[G % 2], 64 * (G // 2))
                nc.scalar.activation(nmaxT[:, G % 2, :], M1[0:GH * PARTS, 0:S // 2].bitcast(bf16), ACT.Copy).then_inc(nmt_sb, 1)

            def copy_out(G):
                ac.wait_ge(pv_ready, G + 1)
                if G >= 1:
                    ac.wait_ge(ott_ready, G)
                nc.scalar.activation(OT[:, :], O_BANK[:, :], ACT.Copy).then_inc(ot_sb, 1)

            def copy_at(b):
                ac.wait_ge(aot_ready, b + 1)
                if b >= 1:
                    ac.wait_ge(wo_ready, b)
                nc.scalar.activation(AT[:, :], M0[:, :], ACT.Copy).then_inc(at_sb, 1)

            ffn(0)
            NGT = B * NG
            for b in range(2):
                split_xt(ln_index(1, b))
                copy_qk(b, 0)
                copy_qk(b, 1)
                values(b)
            for n in range(-2, NGT + 3):
                nb = n // NG + 1
                fresh = n > 0 and n % NG == 0 and nb < B
                for i in range(NU):
                    if 0 <= n < NGT:
                        exps(n, i)
                    if i == 1 and 0 <= n + 1 < NGT:
                        copy_nmax(n + 1)
                    if i == 2 and fresh:
                        split_xt(ln_index(1, nb))
                    if i in (5, 7) and fresh:
                        copy_qk(nb, (i - 5) // 2)
                    if i == 9 and fresh:
                        values(nb)
                    if i == 6 and n - 2 >= NG - 1 and (n - 2) % NG == NG - 1 and (n - 2) // NG < B:
                        copy_at((n - 2) // NG)
                if 0 <= n - 1 < NGT:
                    copy_out(n - 1)
            ffn(1)

        @block.vector
        def _(v):
            count = [0]

            def link(ins):
                count[0] += 1
                ins.then_inc(dve_chain, 1)
                v.wait_ge(dve_chain, count[0])

            def layer_norm(kind, b):
                n = ln_index(kind, b)
                xt = X[:, b * NT:(b + 1) * NT, :]
                for t in range(NT):
                    i = nc.vector.bn_stats(stats[:, t, :], xt[:, t, :])
                link(i)
                for t in range(NT):
                    i = nc.vector.bn_aggr(mv[:, t, :], stats[:, t, :])
                link(i)
                link(nc.vector.tensor_scalar(vhalf[:, :], mv[:, :, 1], EPS, None, ALU.add))
                link(nc.vector.tensor_scalar(rstd[:, :].bitcast(i32), vhalf[:, :].bitcast(i32), -0.5, RSQRT_MAGIC, ALU.mult, ALU.add))
                link(nc.vector.tensor_scalar(vhalf[:, :], vhalf[:, :], -0.5, None, ALU.mult))
                for _ in range(3):
                    link(nc.vector.tensor_tensor(newton[:, :], rstd[:, :], vhalf[:, :], ALU.mult))
                    link(nc.vector.tensor_tensor(newton[:, :], newton[:, :], rstd[:, :], ALU.mult))
                    link(nc.vector.scalar_tensor_tensor(rstd[:, :], newton[:, :], 1.5, rstd[:, :], ALU.add, ALU.mult))
                if n >= 1:
                    v.wait_ge(xt_ready, n)
                for t in range(NT):
                    i = nc.vector.tensor_scalar(XN[:, t, :], xt[:, t, :], mv[:, t, 0:1], rstd[:, t:t + 1],
                                                ALU.subtract, ALU.mult)
                i.then_inc(xn_ready, 1)

            def split_xt(n):
                v.wait_ge(xh_ready, n + 1)
                nc.vector.tensor_tensor(XL[:, n % 2, :], M0[:, :], XH[:, n % 2, :], ALU.subtract).then_inc(xl_ready, 1)

            lg = M0[:, 0:10 * NT].rearrange("p (t e) -> p t e", e=10)

            def router_shift(j):
                v.wait_ge(lg_ready, j + 1)
                link(nc.vector.tensor_reduce(nmx[:, :], lg[:, :, 0:E], AX.X, ALU.max, negate=True))
                nc.vector.tensor_tensor(shifted[:, :, :], lg[:, :, 0:E],
                                        nmx[:, :].unsqueeze(2).broadcast_to([P, NT, E]), ALU.add).then_inc(shift_ready, 1)

            def route(j):
                v.wait_ge(ex_ready, 2 * (j + 1))
                nc.vector.tensor_reduce(ssum[:, :], ex[:, :, :], AX.X, ALU.add).then_inc(dve_chain, 1)
                count[0] += 1
                other = ex[:, :, :].unsqueeze(2).broadcast_to([P, NT, E, E])
                own = ex[:, :, :].unsqueeze(3).broadcast_to([P, NT, E, E])
                nc.vector.tensor_tensor(above[:, :, :, :], other, own, ALU.is_gt).then_inc(dve_chain, 1)
                count[0] += 1
                link(nc.vector.tensor_tensor(level[:, :, :, :], other, own, ALU.is_ge))
                link(nc.vector.tensor_tensor(level[:, :, :, :], level[:, :, :, :],
                                             earlier_sb[:, :, :].unsqueeze(1).broadcast_to([P, NT, E, E]), ALU.mult))
                link(nc.vector.tensor_tensor(above[:, :, :, :], above[:, :, :, :], level[:, :, :, :], ALU.max))
                link(nc.vector.tensor_reduce(rank[:, :, :], above[:, :, :, :], AX.X, ALU.add))
                link(nc.vector.reciprocal(rsum[:, :], ssum[:, :]))
                link(nc.vector.scalar_tensor_tensor(kept[:, :, :], rank[:, :, :], 1.5, ex[:, :, :], ALU.is_lt, ALU.mult))
                nc.vector.tensor_scalar(coef[:, :, E], th[:, :], 1.0, 0.25, ALU.add, ALU.mult).then_inc(dve_chain, 1)
                count[0] += 1
                link(nc.vector.scalar_tensor_tensor(coef[:, :, 0:E], kept[:, :, :], 0.5,
                                                    rsum[:, :].unsqueeze(2).broadcast_to([P, NT, E]), ALU.mult, ALU.mult))
                if j >= 1:
                    v.wait_ge(ct_ready, j)
                link(nc.vector.tensor_copy(coef3[:, :, 0, :], coef[:, :, :]))
                link(nc.vector.tensor_tensor(rest[:, :, :], coef[:, :, :], coef3[:, :, 0, :], ALU.subtract))
                link(nc.vector.tensor_copy(coef3[:, :, 1, :], rest[:, :, :]))
                nc.vector.tensor_tensor(coef3[:, :, 2, :], rest[:, :, :], coef3[:, :, 1, :], ALU.subtract).then_inc(c3_ready, 1)

            def copy_ct(j):
                v.wait_ge(ct_ready, j + 1)
                nc.vector.tensor_copy(coefT[:, j % 2, :], M0[0:PARTS * C, 0:S // 2].bitcast(bf16)).then_inc(ct_sb, 1)

            def expert(i):
                j, n = divmod(i, C)
                v.wait_ge(act_ready, i + 1)
                v.wait_ge(c_ready, i + 1)
                if i >= 3:
                    v.wait_ge(y_step, i - 2)
                a = act[:, i % 3, :]
                if n == E:
                    v.wait_ge(h_ready, HID * (j + 1))
                    nc.vector.tensor_tensor(gated[:, :], a, H_BANK[(HID * j + E + 1) % 3][:, :], ALU.mult).then_inc(up_used, 1)
                    v.wait_ge(up_used, j + 1)
                    a = gated[:, :]
                nc.vector.tensor_tensor(hid[:, i % 3, :], a, C_BANK[i % 2][:, :], ALU.mult).then_inc(hid_ready, 1)

            def add_ffn(j):
                b = j % B
                v.wait_ge(ytt_ready, j + 1)
                xt = X[:, b * NT:(b + 1) * NT, :]
                nc.vector.tensor_tensor(xt, xt, M1[:, :].rearrange("p (t d) -> p t d", t=NT), ALU.add).then_inc(x_ffn, 1)

            def ffn(kind):
                if kind == 0:
                    v.wait_ge(ld_c, 64)
                    v.wait_ge(ld_x[0], 16)
                layer_norm(2 * kind, 0)
                if kind == 0:
                    split_weights(0)
                split_xt(ln_index(2 * kind, 0))
                if kind == 0:
                    split_weights(1)
                router_shift(B * kind)
                route(B * kind)
                copy_ct(B * kind)
                for b in range(B):
                    j = B * kind + b
                    for n in range(C):
                        expert(C * j + n)
                        if n == 0 and b >= 1:
                            add_ffn(j - 1)
                        if n == 1 and b + 1 < B:
                            if kind == 0:
                                v.wait_ge(ld_x[b + 1], 16)
                            layer_norm(2 * kind, b + 1)
                        if n == 4 and b + 1 < B:
                            split_xt(ln_index(2 * kind, b + 1))
                        if n == 5 and b + 1 < B:
                            router_shift(j + 1)
                        if n == 7 and b + 1 < B:
                            route(j + 1)
                    if b + 1 < B:
                        copy_ct(j + 1)
                add_ffn(B * kind + B - 1)

            def split_weights(k):
                cut = [(rt_raw[:, :], rt_hi[:, :], rt_lo[:, :])] if k == 0 else []
                n0, n1 = ((0, 0), (0, (E + 2) * F), ((E + 2) * F, NW))[k]
                if n1 > n0:
                    cut += [(w_raw[:, n0:n1], w_hi[:, n0:n1], w_lo[:, n0:n1])]
                v.wait_ge(ld_w if k < 2 else ld_wa, 16 * (2 + E) if k < 2 else 48)
                for raw, hi, lo in cut:
                    link(nc.vector.tensor_copy(hi, raw))
                    nc.vector.tensor_tensor(lo, raw, hi, ALU.subtract).then_inc(w_split, 1)

            def qk_split(b, i):
                v.wait_ge(qk_sb, 2 * b + i + 1)
                if b >= 1:
                    v.wait_ge((scr_q, scr_k)[i], 48 * b)
                p = qk_parts[:, i]
                link(nc.vector.tensor_copy(p[:, 0, :], qk_f[:, i, :]))
                link(nc.vector.tensor_tensor(qk_rest[:, i, :], qk_f[:, i, :], p[:, 0, :], ALU.subtract))
                link(nc.vector.tensor_copy(p[:, 1, :], qk_rest[:, i, :]))
                nc.vector.tensor_tensor(p[:, 2, :], qk_rest[:, i, :], p[:, 1, :], ALU.subtract).then_inc(parts_ready, 1)

            def maxima(G, i):
                u = NU * G + i
                v.wait_ge(s_ready, u + 1)
                a = score_units(G % NG)[i]
                bank = S_BANK[u % 2]
                hh = a[0][1] - GH * (G % NG)
                dst = nmax[:, G % 2]
                if a[0][2] == 1:
                    r = nc.vector.tensor_reduce(dst[:, hh:hh + 3:2, 1], bank[:, :].rearrange("p (h n) -> p h n", h=2),
                                                AX.X, ALU.max, negate=True)
                else:
                    for off, _, qt in a:
                        r = nc.vector.tensor_reduce(dst[:, hh, qt:qt + 1], bank[:, off:off + (qt + 1) * P],
                                                    AX.X, ALU.max, negate=True)
                r.then_inc(s_used, 1)

            def split_nmax(G):
                v.wait_ge(s_used, NU * (G + 1))
                if G >= 1:
                    v.wait_ge(nmt_ready, G)
                m = nmax[:, G % 2].rearrange("p h t -> p t h")
                r = nmax_rest[:, :, :].rearrange("p h t -> p t h")
                link(nc.vector.tensor_copy(nmax3[:, :, :, 0], m))
                link(nc.vector.tensor_tensor(r, m, nmax3[:, :, :, 0], ALU.subtract))
                link(nc.vector.tensor_copy(nmax3[:, :, :, 1], r))
                nc.vector.tensor_tensor(nmax3[:, :, :, 2], r, nmax3[:, :, :, 1], ALU.subtract).then_inc(nm3_ready, 1)

            def normalise(G):
                g = G % NG
                v.wait_ge(ott_ready, G + 1)
                o = M1[:, :].rearrange("p (t h c) -> p t h c", t=NT, h=GH)
                link(nc.vector.reciprocal(rden[:, :, :], o[:, :, :, HD]))
                if g == 0 and G >= NG:
                    v.wait_ge(aot_ready, G // NG)
                dst = AO[:, :, GH * HD * g:GH * HD * (g + 1)].rearrange("p t (h d) -> p t h d", d=HD)
                i = nc.vector.tensor_tensor(dst, o[:, :, :, 0:HD], rden[:, :, :].unsqueeze(3).broadcast_to([P, NT, GH, HD]),
                                            ALU.mult)
                i.then_inc(ott_used, 1)

            def add_attention(b):
                v.wait_ge(wo_ready, b + 1)
                xt = X[:, b * NT:(b + 1) * NT, :]
                nc.vector.tensor_tensor(xt, xt, M0[:, :].rearrange("p (t d) -> p t d", t=NT), ALU.add).then_inc(x_att, 1)

            ffn(0)
            split_weights(2)
            NGT = B * NG
            for b in range(2):
                v.wait_ge(x_ffn, b + 1)
                layer_norm(1, b)
                split_xt(ln_index(1, b))
                qk_split(b, 0)
                qk_split(b, 1)
            for n in range(-2, NGT + 3):
                nb = n // NG + 1
                fresh = n > 0 and n % NG == 0 and nb < B
                done = (n - 2) // NG if n - 2 >= NG - 1 and (n - 2) % NG == NG - 1 and (n - 2) // NG < B else None
                if fresh:
                    v.wait_ge(x_ffn, nb + 1)
                    layer_norm(1, nb)
                for i in range(NU):
                    if 0 <= n + 2 < NGT:
                        maxima(n + 2, i)
                    if i == 3 and 0 <= n - 2 < NGT:
                        normalise(n - 2)
                    if i == 3 and fresh:
                        split_xt(ln_index(1, nb))
                    if i in (6, 8) and fresh:
                        qk_split(nb, (i - 6) // 2)
                if 0 <= n + 2 < NGT:
                    split_nmax(n + 2)
                if done is not None:
                    add_attention(done)
            v.wait_ge(x_att, B)
            ffn(1)

        @block.tensor
        def _(pe):
            def three_pass(dst, w_h, w_l, m_h, m_l):
                nc.tensor.matmul(dst, w_h, m_h, start=True, stop=False)
                nc.tensor.matmul(dst, w_h, m_l, start=False, stop=False)
                return nc.tensor.matmul(dst, w_l, m_h, start=False, stop=True)

            def transpose_xn(n, free):
                pe.wait_ge(xn_ready, n + 1)
                for s, c in free:
                    pe.wait_ge(s, c)
                for t in range(NT):
                    i = nc.tensor.transpose(M0[:, t * P:(t + 1) * P], XN[:, t, :], id_f[:, :])
                i.then_inc(xt_ready, 1)

            def logits(j, n):
                pe.wait_ge(xl_ready, n + 1)
                for t in range(NT):
                    c = slice(t * P, (t + 1) * P)
                    i = three_pass(M0[:, 10 * t:10 * t + 10], XH[:, n % 2, c], XL[:, n % 2, c], rt_hi[:, :], rt_lo[:, :])
                i.then_inc(lg_ready, 1)

            def transpose_coef(j):
                pe.wait_ge(c3_ready, j + 1)
                pe.wait_ge(ex_ready, 2 * (j + 1))
                dst = M0[0:PARTS * C, 0:S // 2].bitcast(bf16)
                for t in range(NT):
                    i = nc.tensor.transpose(dst[:, t * P:(t + 1) * P],
                                            coef3[:, t, :, :].rearrange("p a c -> p (a c)"), id_b[:, :])
                i.then_inc(ct_ready, 1)

            def hidden(j, n, ln):
                i = HID * j + n
                if i >= 3:
                    jj, nn = divmod(i - 3, HID)
                    if nn == E + 1:
                        pe.wait_ge(up_used, jj + 1)
                    else:
                        pe.wait_ge(act_ready, C * jj + nn + 1)
                c = slice(n * F, (n + 1) * F)
                three_pass(H_BANK[i % 3][:, :], w_hi[:, c], w_lo[:, c], XH[:, ln % 2, :], XL[:, ln % 2, :]).then_inc(h_ready, 1)

            def spread(j, n):
                i = C * j + n
                if i >= 2:
                    pe.wait_ge(hid_ready, i - 1)
                nc.tensor.matmul(C_BANK[i % 2][:, :], sel_sb[:, n, :], coefT[:, j % 2, :], start=True, stop=True).then_inc(c_ready, 1)

            def combine(j, n):
                i = C * j + n
                pe.wait_ge(hid_ready, i + 1)
                if n == 0 and j >= 1:
                    pe.wait_ge(yt_sb, j)
                m = nc.tensor.matmul(Y_BANK[:, :], w2_sb[:, n, :], hid[:, i % 3, :], start=(n == 0), stop=(n == E))
                m.then_inc(y_step, 1)

            def transpose_y(j):
                pe.wait_ge(yt_sb, j + 1)
                if j >= 1:
                    pe.wait_ge(x_ffn, j)
                for t in range(NT):
                    i = nc.tensor.transpose(M1[:, t * P:(t + 1) * P], YT[:, t * P:(t + 1) * P], id_f[:, :])
                i.then_inc(ytt_ready, 1)

            def ffn(kind):
                ln = ln_index(2 * kind, 0)
                transpose_xn(ln, [])
                if kind == 0:
                    pe.wait_ge(w_split, 1)
                logits(B * kind, ln)
                transpose_coef(B * kind)
                for b in range(B):
                    j, ln = B * kind + b, ln_index(2 * kind, b)
                    if kind == 0 and b == 0:
                        pe.wait_ge(w_split, 2)
                    pe.wait_ge(ct_sb, j + 1)
                    hidden(j, 0, ln)
                    spread(j, 0)
                    hidden(j, 1, ln)
                    spread(j, 1)
                    if b >= 1:
                        transpose_y(j - 1)
                    for n in range(C):
                        if n + 2 < HID:
                            hidden(j, n + 2, ln)
                        if n + 2 < C:
                            spread(j, n + 2)
                        if j == 0 and n == 0:
                            pe.wait_ge(ld_w2, 32)
                        combine(j, n)
                        if b + 1 < B:
                            if n == 1:
                                transpose_xn(ln + 1, [(ct_sb, j + 1)])
                            if n == 5:
                                logits(j + 1, ln + 1)
                    if b + 1 < B:
                        transpose_coef(j + 1)
                transpose_y(B * kind + B - 1)

            def attention_xn(b):
                transpose_xn(ln_index(1, b), [[], [(v_sb, 1)], [(v_sb, 2)]][b] if b < 3 else [(x_att, b - 2)])

            def project(b, i):
                ln = ln_index(1, b)
                if i == 0:
                    pe.wait_ge(xl_ready, ln + 1)
                else:
                    pe.wait_ge(qk_sb, 2 * b + 1)
                c = slice((E + 2) * F + i * D, (E + 2) * F + (i + 1) * D)
                three_pass(M0[:, :], w_hi[:, c], w_lo[:, c], XH[:, ln % 2, :], XL[:, ln % 2, :]).then_inc(qk_ready, 1)

            def values(b):
                ln = ln_index(1, b)
                c = slice((E + 2) * F + 2 * D, (E + 2) * F + 3 * D)
                pe.wait_ge(qk_sb, 2 * b + 2)
                for t in range(NT):
                    r = slice(t * P, (t + 1) * P)
                    m = three_pass(M0[:, r], XH[:, ln % 2, r], XL[:, ln % 2, r], w_hi[:, c], w_lo[:, c])
                m.then_inc(v_ready, 1)

            def scores(G, i):
                b, g = divmod(G, NG)
                u = NU * G + i
                if u >= 2:
                    pe.wait_ge(s_used, u - 1)
                if i == 0 and g == 0:
                    pe.wait_ge(qa_ready[b % 2], 32 * (b // 2 + 1))
                    pe.wait_ge(ka_ready[b % 2], 32 * (b // 2 + 1))
                for off, h, qt in score_units(g)[i]:
                    lo = 64 * (h % 2)
                    r = slice(lo, lo + ROWS_S)
                    dst = S_BANK[u % 2]
                    n = (qt + 1) * P
                    nc.tensor.matmul(dst[:, off:off + n], QA[b % 2][r, h // 2, qt * P:(qt + 1) * P],
                                     KA[b % 2][r, h // 2, 0:n], start=True, stop=False, skip_group_check=True)
                    m = nc.tensor.matmul(dst[:, off + qt * P:off + n], id_b[:, :], causal_sb[:, :],
                                         start=False, stop=True, skip_group_check=True)
                m.then_inc(s_ready, 1)

            def transpose_nmax(G):
                pe.wait_ge(nm3_ready, G + 1)
                if G >= 4:
                    pe.wait_ge(ott_used, G - 3)
                dst = M1[0:GH * PARTS, 0:S // 2].bitcast(bf16)
                for t in range(NT):
                    i = nc.tensor.transpose(dst[:, t * P:(t + 1) * P], nmax3[:, t, :, :].rearrange("p h a -> p (h a)"), id_b[:, :])
                i.then_inc(nmt_ready, 1)

            def scores_t(G, i):
                b, g = divmod(G, NG)
                u = NU * G + i
                if i == 0:
                    pe.wait_ge(nm_rows[G % 2], 64 * (G // 2 + 1))
                if u >= 3:
                    pe.wait_ge(exp_done, u - 2)
                for off, h, kt in prob_units(g)[i]:
                    lo = 64 * (h % 2)
                    r = slice(lo, lo + ROWS_T)
                    m = nc.tensor.matmul(T_BANK[u % 3][:, off:off + WID[kt]], KA[b % 2][r, h // 2, kt * P:(kt + 1) * P],
                                         QA[b % 2][r, h // 2, kt * P:S], start=True, stop=True, skip_group_check=True)
                m.then_inc(t_ready, 1)

            def weigh_values(G, k):
                b, g = divmod(G, NG)
                kt = k
                pe.wait_ge(masked, NT * G + {0: 1, 3: 2, 1: 3, 2: 4}[kt])
                if k == 0:
                    if G >= 1:
                        pe.wait_ge(ot_sb, G)
                    if g == 0:
                        pe.wait_ge(v_sb, b + 1)
                for hh in range(GH):
                    m = nc.tensor.matmul(O_BANK[32 * hh:32 * hh + 32, kt * P:S], VA[b % 2][:, kt, GH * g + hh, :],
                                         probs[G % 2][:, hh, POS[kt]:POS[kt] + WID[kt]],
                                         start=(k == 0), stop=(k == NT - 1), skip_group_check=True)
                if k == NT - 1:
                    m.then_inc(pv_ready, 1)

            def transpose_out(G):
                pe.wait_ge(ot_sb, G + 1)
                if G + 3 < B * NG:
                    pe.wait_ge(nmt_sb, G + 4)
                elif G >= 1:
                    pe.wait_ge(ott_used, G)
                for t in range(NT):
                    i = nc.tensor.transpose(M1[:, t * P:(t + 1) * P], OT[:, t * P:(t + 1) * P], id_f[:, :])
                i.then_inc(ott_ready, 1)

            def transpose_ao(b):
                pe.wait_ge(ott_used, NG * (b + 1))
                pe.wait_ge(v_sb, min(b + 3, B))
                if b >= 1:
                    pe.wait_ge(x_att, b)
                for t in range(NT):
                    i = nc.tensor.transpose(M0[:, t * P:(t + 1) * P], AO[:, t, :], id_f[:, :])
                i.then_inc(aot_ready, 1)

            def output(b):
                pe.wait_ge(at_sb, b + 1)
                for t in range(NT):
                    m = nc.tensor.matmul(M0[:, t * P:(t + 1) * P], AT[:, t * P:(t + 1) * P], wo_sb[:, :], start=True, stop=True)
                m.then_inc(wo_ready, 1)

            pe.wait_ge(ld_c, 64)
            ffn(0)
            pe.wait_ge(x_ffn, B)
            NGT = B * NG
            pe.wait_ge(w_split, 3)
            pe.wait_ge(ld_ac, 16 * 10)
            for b in range(2):
                attention_xn(b)
                project(b, 0)
                project(b, 1)
                values(b)
            for n in range(-2, NGT + 3):
                nb = n // NG + 1
                fresh = n > 0 and n % NG == 0 and nb < B
                done = (n - 2) // NG if n - 2 >= NG - 1 and (n - 2) % NG == NG - 1 and (n - 2) // NG < B else None
                for i in range(NU):
                    if 0 <= n < NGT:
                        scores_t(n, i)
                    if 0 <= n + 2 < NGT:
                        scores(n + 2, i)
                    if i == 0 and 0 <= n + 1 < NGT:
                        transpose_nmax(n + 1)
                    if i == 2 and 0 <= n - 2 < NGT:
                        transpose_out(n - 2)
                    if i in (1, 4, 6, 8) and 0 <= n - 1 < NGT:
                        weigh_values(n - 1, (1, 4, 6, 8).index(i))
                    if i == 1 and fresh:
                        attention_xn(nb)
                    if i in (4, 6) and fresh:
                        project(nb, (i - 4) // 2)
                    if i == 8 and fresh:
                        values(nb)
                    if i == 5 and done is not None:
                        transpose_ao(done)
                    if i == 7 and done is not None:
                        output(done)
            pe.wait_ge(x_att, B)
            ffn(1)


def kernel(**inputs):
    import numpy as np
    import ml_dtypes
    import concourse.bacc as bacc
    from concourse import mybir
    from concourse.bass_utils import run_bass_kernel_spmd as run

    bf = ml_dtypes.bfloat16
    H, S, E, P = 16, 512, 8, 128
    slopes = np.array([1.0 / ((2.0 ** 8) ** (1.0 / H)) ** (i + 1) for i in range(H)], np.float32)

    def parts(a):
        out, rest = [], np.asarray(a, np.float64)
        for _ in range(3):
            out.append(rest.astype(np.float32).astype(bf))
            rest = rest - out[-1].astype(np.float64)
        return out

    lift = slopes.astype(np.float64)[:, None] * np.arange(S)
    ones = [np.ones((H, S), bf)]
    by_pair = lambda rows: np.ascontiguousarray(np.stack(rows).reshape(len(rows), H // 2, 2, S).transpose(2, 0, 1, 3))
    select = np.zeros((3, E + 1, E + 1, P), bf)
    for e in range(E + 1):
        select[:, e, e, :] = 1
    a = {k: np.asarray(v) for k, v in inputs.items()}
    arrays = {
        "x": a["L0_attn_x"],
        "w1": a["L0_ffn_w1"],
        "w2": a["L0_ffn_w2"],
        "gate_up": a["L0_ffn_shared_gate_up"],
        "down": a["L0_ffn_shared_down"],
        "router": np.concatenate([a["L0_ffn_router_w"], a["L0_ffn_shared_gate_w"], np.zeros((P, 1), np.float32)], 1),
        "wq": a["L0_attn_Wq"].T, "wk": a["L0_attn_Wk"].T, "wv": a["L0_attn_Wv"].T, "wo": a["L0_attn_Wo"].T,
        "q_const": by_pair(ones * 3 + parts(lift)),
        "k_const": by_pair(parts(-lift) + ones * 6),
        "select": select.reshape(3 * (E + 1), E + 1, P),
        "earlier": np.tril(np.ones((E, E), np.float32), -1),
        "causal": np.triu(np.full((P, P), -1e30, np.float32), 1).astype(bf),
        "ident": np.eye(P, dtype=np.float32),
        "ident_b": np.eye(P, dtype=np.float32).astype(bf),
    }
    nc = bacc.Bacc("TRN2", target_bir_lowering=False, num_devices=1)
    data, args = {}, []
    for name, v in arrays.items():
        v = np.ascontiguousarray(v)
        data["in_" + name] = v
        args.append(nc.dram_tensor("in_" + name, v.shape, mybir.dt.from_np(v.dtype), kind="ExternalInput").ap())
    args.append(nc.dram_tensor("out_x", a["L0_attn_x"].shape, mybir.dt.float32, kind="ExternalOutput").ap())
    macaron_block(nc, *args)
    r = run(nc, [data], core_ids=[0])
    return r.results[0]["out_x"]
```

```python
import concourse.bass as bass
from concourse import mybir
from contextlib import ExitStack


def macaron_block(nc: bass.Bass, x, w1, w2, gate_up, down, router, wq, wk, wv, wo,
                  q_const, k_const, least, causal, ident, ident_b, out):
    f32, f32r, bf16 = mybir.dt.float32, mybir.dt.float32r, mybir.dt.bfloat16
    i32 = mybir.dt.int32
    ALU, ACT, AX = mybir.AluOpType, mybir.ActivationFunctionType, mybir.AxisListType

    P = 128
    B, S, D = x.shape
    E, _, F = w1.shape
    NT = S // P
    H, HD = 16, D // 16
    NP = H // 2
    GH = 4
    NG = H // GH
    C = E + 1
    PARTS = 3
    PROD = 6 * HD
    ROWS_S, ROWS_T = PROD + 6, PROD + 9
    VW = 32
    EPS = 1e-5
    RSQRT_MAGIC = float(0x5F3759DF)
    SPAN = 1280
    WID = [S - P * kt for kt in range(NT)]

    ctx = ExitStack()
    with ctx:
        def sb(name, shape, dt=f32):
            return ctx.enter_context(nc.sbuf_tensor(name, shape, dt))

        def sem(name):
            return ctx.enter_context(nc.semaphore(name))

        NW = E * F + 2 * F + 3 * D
        w_raw = sb("w_raw", [P, NW])
        w_hi, w_lo = sb("w_hi", [P, NW], f32r), sb("w_lo", [P, NW], f32r)
        rt_raw, rt_hi, rt_lo = sb("rt_raw", [P, 10]), sb("rt_hi", [P, 10], f32r), sb("rt_lo", [P, 10], f32r)
        w2_sb = sb("w2_sb", [P, C, D])
        wo_sb = sb("wo_sb", [P, D])
        id_f, id_b = sb("id_f", [P, P]), sb("id_b", [P, P], bf16)
        least_lead = sb("least_lead", [P, E, E])
        causal_sb = sb("causal_sb", [P, P], bf16)
        X = sb("X", [P, B * NT, D])
        stats, mv, rstd = sb("stats", [P, NT, 6]), sb("mv", [P, NT, 2]), sb("rstd", [P, NT])
        vhalf, newton = sb("vhalf", [P, NT]), sb("newton", [P, NT])
        XN = sb("XN", [P, 2, NT, D])
        XH, XL = sb("XH", [P, 3, S], f32r), sb("XL", [P, 3, S], f32r)
        table = sb("table", [P, 3])
        nmx, shifted, ex = sb("nmx", [P, NT]), sb("shifted", [P, NT, E]), sb("ex", [P, NT, E])
        sl = sb("sl", [P, NT, E])
        th, ssum, rsum = sb("th", [P, NT]), sb("ssum", [P, NT]), sb("rsum", [P, NT])
        above, lead = sb("above", [P, NT, E, E]), sb("lead", [P, NT, E, E])
        kept, coef = sb("kept", [P, NT, E]), sb("coef", [P, 2, NT, C])
        rest = sb("rest", [P, NT, E])
        act = sb("act", [P, 3, S])
        gated = sb("gated", [P, S])
        qk_rest = sb("qk_rest", [P, 2, S])
        qk_parts = sb("qk_parts", [P, 2, PARTS, S], bf16)
        QA = [sb(f"QA{i}", [P, NP, S], bf16) for i in range(2)]
        KA = [sb(f"KA{i}", [P, NP, S], bf16) for i in range(2)]
        VA = [sb(f"VA{i}", [P, NT, H, VW]) for i in range(2)]
        nmax = sb("nmax", [P, 2, GH, NT])
        nmax_rest = sb("nmax_rest", [P, GH, NT])
        nmax3 = sb("nmax3", [P, NT, GH, PARTS], bf16)
        nmaxT = sb("nmaxT", [GH * PARTS, 2, S], bf16)
        probs = [sb(f"probs{i}", [P, GH, SPAN]) for i in range(2)]
        OT = sb("OT", [P, S])
        rden = sb("rden", [P, NT, GH])
        AO = sb("AO", [P, NT, D])
        AT = sb("AT", [P, S])
        scratch = nc.dram_tensor("qk_scratch", [2, B, P, 6, S], bf16, kind="Internal").ap()

        banks = [ctx.enter_context(nc.psum_tensor(f"bank{i}", [P, S], f32)) for i in range(8)]
        H_BANK, Y_BANK, M0, M1 = banks[0:3], banks[3:6], banks[6], banks[7]
        S_BANK, T_BANK, O_BANK, MISC = [banks[0], banks[1], banks[7]], banks[2:5], banks[5], banks[6]

        ld_x = [sem(f"ld_x{b}") for b in range(B)]
        ld_w = [sem(f"ld_weights{k}") for k in range(5)]
        ld_c, ld_cf, ld_w2, ld_ac = sem("ld_c"), sem("ld_cf"), sem("ld_w2"), sem("ld_ac")
        w_high, w_split = sem("w_high"), sem("w_split")
        va_set = sem("va_set")
        mv_ready = sem("mv_ready")
        xn_ready, xt_ready, xh_ready, xl_ready = sem("xn_ready"), sem("xt_ready"), sem("xh_ready"), sem("xl_ready")
        lg_ready, shift_ready, ex_ready = sem("lg_ready"), sem("shift_ready"), sem("ex_ready")
        sm_ready, lead_ready, above_ready = sem("sm_ready"), sem("lead_ready"), sem("above_ready")
        coef_ready = sem("coef_ready")
        h_ready, act_ready, up_used = sem("h_ready"), sem("act_ready"), sem("up_used")
        y_ready, y_used = sem("y_ready"), sem("y_used")
        qk_ready, qk_high, qk_sub = sem("qk_ready"), sem("qk_high"), sem("qk_sub")
        mid_qk, parts_ready = sem("mid_qk"), sem("parts_ready")
        v_ready, v_sb = sem("v_ready"), sem("v_sb")
        scr_q, scr_k = sem("scr_q"), sem("scr_k")
        qa_ready, ka_ready = [sem("qa_ready0"), sem("qa_ready1")], [sem("ka_ready0"), sem("ka_ready1")]
        ao_ready, aot_ready, at_sb, wo_ready, x_att = sem("ao_ready"), sem("aot_ready"), sem("at_sb"), sem("wo_ready"), sem("x_att")
        s_ready, s_used = sem("s_ready"), sem("s_used")
        nm3_ready, nmt_ready, nmt_sb = sem("nm3_ready"), sem("nmt_ready"), sem("nmt_sb")
        nm_rows = [sem("nm_rows0"), sem("nm_rows1")]
        t_ready, exp_done, masked = sem("t_ready"), sem("exp_done"), sem("masked")
        pv_ready, ot_sb, ott_ready, ott_used = sem("pv_ready"), sem("ot_sb"), sem("ott_ready"), sem("ott_used")
        stored = sem("stored")
        dve_chain, act_chain, pool_chain = sem("dve_chain"), sem("act_chain"), sem("pool_chain")

        block = ctx.enter_context(nc.Block())

        NJ = 2 * B
        HID = E + 2
        LATER = (((0, 2), None), ((0, 3), (1, 0)), (None, (1, 1)), ((1, 2), None)), \
                (((2, 2), None), ((2, 3), None), (None, None), (None, None))
        CUTS = ((0, 2 * F), (2 * F, 6 * F), (6 * F, (E + 2) * F), ((E + 2) * F, NW))
        NU = 10

        def ln_index(kind, b):
            return kind * B + b

        def rsqrt(engine, link):
            link(engine.tensor_scalar(vhalf[:, :], mv[:, :, 1], EPS, None, ALU.add))
            link(engine.tensor_scalar(rstd[:, :].bitcast(i32), vhalf[:, :].bitcast(i32), -0.5, RSQRT_MAGIC, ALU.mult, ALU.add))
            link(engine.tensor_scalar(vhalf[:, :], vhalf[:, :], -0.5, None, ALU.mult))
            for _ in range(3):
                link(engine.tensor_tensor(newton[:, :], rstd[:, :], vhalf[:, :], ALU.mult))
                link(engine.tensor_tensor(newton[:, :], newton[:, :], rstd[:, :], ALU.mult))
                link(engine.tensor_scalar(newton[:, :], newton[:, :], 1.5, None, ALU.add))
                link(engine.tensor_tensor(rstd[:, :], newton[:, :], rstd[:, :], ALU.mult))

        def score_units(g):
            heads = range(GH * g, GH * g + GH)
            return ([[(0, h, 3)] for h in heads] + [[(0, h, 2), (3 * P, h, 0)] for h in heads]
                    + [[(0, h, 1), (2 * P, h + 2, 1)] for h in heads[:2]])

        def prob_units(g):
            heads = range(GH * g, GH * g + GH)
            return ([[(0, h, 0)] for h in heads] + [[(0, h, 3), (P, h, 1)] for h in heads]
                    + [[(0, h, 2), (2 * P, h + 2, 2)] for h in heads[:2]])

        POS = {0: 0, 3: 512, 1: 640, 2: 1024}
        NGT = B * NG

        STEPS = range(-2, NGT + 1)
        QK_SCALE = (float(HD) ** -0.5, 1.0)

        def batch_at(n, phase):
            b, rest = divmod(n + 7 - phase, NG)
            return b if rest == 0 and 2 <= b < B else None


        def batch_done(n):
            b, rest = divmod(n - 5, NG)
            return b if rest == 0 and 0 <= b < B else None

        @block.sync
        def _(sp):
            for t in (0, 1):
                sp.dma_start(X[:, t, :], x[0, t * P:(t + 1) * P, :]).then_inc(ld_x[0], 16)
            sp.dma_start(w_raw[:, 0:2 * F].rearrange("p (e f) -> p e f", f=F),
                         w1[0:2].rearrange("e d f -> d e f")).then_inc(ld_w[1], 16)
            sp.dma_start(w_raw[:, 2 * F:6 * F].rearrange("p (e f) -> p e f", f=F),
                         w1[2:6].rearrange("e d f -> d e f")).then_inc(ld_w[2], 16)
            sp.dma_start(w2_sb[:, 0:E, :], w2.rearrange("e f d -> f e d")).then_inc(ld_w2, 16)
            sp.dma_start(w_raw[:, 6 * F:E * F].rearrange("p (e f) -> p e f", f=F),
                         w1[6:E].rearrange("e d f -> d e f")).then_inc(ld_w[3], 16)
            sp.dma_start(w_raw[:, E * F:(E + 2) * F], gate_up).then_inc(ld_w[3], 16)
            sp.dma_start(w2_sb[:, E, :], down).then_inc(ld_w2, 16)
            for b in range(1, B):
                sp.dma_start(X[:, b * NT:(b + 1) * NT, :], x[b].rearrange("(t p) d -> p t d", p=P)).then_inc(ld_x[b], 16)
            for i, w in enumerate((wq, wk, wv)):
                sp.dma_start(w_raw[:, (E + 2) * F + i * D:(E + 2) * F + (i + 1) * D], w).then_inc(ld_w[4], 16)
            sp.dma_start(id_b[:, :], ident_b).then_inc(ld_ac, 16)
            sp.dma_start(wo_sb[:, :], wo).then_inc(ld_ac, 16)
            sp.dma_start(causal_sb[:, :], causal).then_inc(ld_ac, 16)
            for i in range(2):
                for par in range(2):
                    sp.dma_start(QA[i][64 * par + PROD:64 * par + PROD + 6, :, :], q_const[par]).then_inc(ld_ac, 16)
                    sp.dma_start(KA[i][64 * par + PROD:64 * par + PROD + 9, :, :], k_const[par]).then_inc(ld_ac, 16)

            def write_parts(b, i):
                sp.wait_ge(parts_ready, 2 * b + i + 1)
                part, dst = qk_parts[:, i], scratch[i, b]
                if i == 0:
                    sp.dma_start(dst[:, 0:3, :], part[:, 0, :].unsqueeze(1).broadcast_to([P, 3, S])).then_inc(scr_q, 16)
                    sp.dma_start(dst[:, 3:5, :], part[:, 1, :].unsqueeze(1).broadcast_to([P, 2, S])).then_inc(scr_q, 16)
                    sp.dma_start(dst[:, 5, :], part[:, 2, :]).then_inc(scr_q, 16)
                else:
                    sp.dma_start(dst[:, 0:3, :], part[:, 0:3, :]).then_inc(scr_k, 16)
                    sp.dma_start(dst[:, 3:5, :], part[:, 0:2, :]).then_inc(scr_k, 16)
                    sp.dma_start(dst[:, 5, :], part[:, 0, :]).then_inc(scr_k, 16)

            def read_rows(b):
                if b >= 2:
                    sp.wait_ge(t_ready, NU * NG * (b - 1))
                for i, (scr, to, ready) in enumerate(((scr_q, QA, qa_ready), (scr_k, KA, ka_ready))):
                    sp.wait_ge(scr, 48 * (b + 1))
                    rows = scratch[i, b].rearrange("(pair par d) s n -> par d s pair n", par=2, d=HD)
                    for par in range(2):
                        sp.dma_start(to[b % 2][64 * par:64 * par + PROD, :, :],
                                     rows[par].rearrange("d s pair n -> (d s) pair n")).then_inc(ready[b % 2], 16)

            def maximum_rows(G):
                b, g = divmod(G, NG)
                sp.wait_ge(nmt_sb, G + 1)
                for hh in range(GH):
                    h = GH * g + hh
                    sp.dma_start(QA[b % 2][64 * (h % 2) + ROWS_S:64 * (h % 2) + ROWS_T, h // 2, :],
                                 nmaxT[PARTS * hh:PARTS * (hh + 1), G % 2, :]).then_inc(nm_rows[G % 2], 16)

            for b in range(2):
                write_parts(b, 0)
                write_parts(b, 1)
                read_rows(b)
            for n in STEPS:
                if (b := batch_at(n, 2)) is not None:
                    write_parts(b, 0)
                if (b := batch_at(n, 3)) is not None:
                    write_parts(b, 1)
                if 0 <= n + 1 < NGT:
                    maximum_rows(n + 1)
                if (b := batch_at(n, 3)) is not None:
                    read_rows(b)
            for b in range(B):
                sp.wait_ge(y_used, C * (B + b + 1))
                sp.dma_start(out[b].rearrange("(t p) d -> p t d", p=P), X[:, b * NT:(b + 1) * NT, :]).then_inc(stored, 16)
            sp.wait_ge(stored, 16 * B)

        @block.gpsimd
        def _(pool):
            count = [0]

            def link(ins):
                count[0] += 1
                ins.then_inc(pool_chain, 1)
                pool.wait_ge(pool_chain, count[0])

            def layer_norm(n, b):
                pool.wait_ge(mv_ready, n + 1)
                rsqrt(nc.gpsimd, link)
                if n >= 2:
                    pool.wait_ge(xt_ready, n - 1)
                link(nc.gpsimd.tensor_tensor(XN[:, n % 2], X[:, b * NT:(b + 1) * NT, :],
                                             mv[:, :, 0:1].broadcast_to([P, NT, D]), ALU.subtract))
                nc.gpsimd.tensor_tensor(XN[:, n % 2], XN[:, n % 2], rstd[:, :].unsqueeze(2).broadcast_to([P, NT, D]),
                                        ALU.mult).then_inc(xn_ready, 1)

            def route(j):
                pool.wait_ge(sm_ready, j + 1)
                other = ex[:, :, :].unsqueeze(2).broadcast_to([P, NT, E, E])
                own = ex[:, :, :].unsqueeze(3).broadcast_to([P, NT, E, E])
                nc.gpsimd.tensor_tensor(lead[:, :, :, :], other, own, ALU.subtract).then_inc(lead_ready, 1)
                pool.wait_ge(above_ready, j + 1)
                half = E // 2
                while half:
                    link(nc.gpsimd.tensor_tensor(above[:, :, :, 0:half], above[:, :, :, 0:half],
                                                 above[:, :, :, half:2 * half], ALU.add))
                    half //= 2
                link(nc.gpsimd.tensor_scalar(kept[:, :, :], above[:, :, :, 0], 1.5, 0.5, ALU.is_lt, ALU.mult))
                link(nc.gpsimd.tensor_tensor(kept[:, :, :], kept[:, :, :], ex[:, :, :], ALU.mult))
                if j >= 2:
                    pool.wait_ge(y_used, C * (j - 1))
                nc.gpsimd.tensor_scalar(coef[:, j % 2, :, E], th[:, :], 1.0, 0.25, ALU.add, ALU.mult)
                nc.gpsimd.tensor_tensor(coef[:, j % 2, :, 0:E], kept[:, :, :],
                                        rsum[:, :].unsqueeze(2).broadcast_to([P, NT, E]), ALU.mult).then_inc(coef_ready, 1)

            def ffn(kind):
                for b in range(B):
                    before, after = LATER[kind][b]
                    if before:
                        layer_norm(ln_index(*before), before[1])
                    if kind == 0 and b == B - 1:
                        for i in range(4):
                            low_qk(i // 2, i % 2)
                    if b + 1 < B:
                        route(B * kind + b + 1)
                    if after:
                        layer_norm(ln_index(*after), after[1])

            layer_norm(1, 1)
            route(0)
            for i in range(2):
                link(nc.gpsimd.memset(VA[i][:, :, :, :], 0.0))
            for i in range(2):
                nc.gpsimd.memset(VA[i][:, :, :, HD:HD + 1], 1.0).then_inc(va_set, 1)

            def low_qk(b, i):
                pool.wait_ge(mid_qk, 2 * b + i + 1)
                nc.gpsimd.tensor_tensor(qk_parts[:, i, 2, :], qk_rest[:, i, :], qk_parts[:, i, 1, :],
                                        ALU.subtract).then_inc(parts_ready, 1)

            def mask(G):
                for kt, need in ((0, 4), (3, 8), (1, 8), (2, 10)):
                    pool.wait_ge(exp_done, NU * G + need)
                    blk = probs[G % 2][:, :, POS[kt]:POS[kt] + P]
                    nc.gpsimd.affine_select(out=blk, in_=blk, compare_op=ALU.is_ge, fill=0.0, base=0,
                                            pattern=[[0, GH], [1, P]], channel_multiplier=-1).then_inc(masked, 1)

            ffn(0)
            for n in STEPS:
                if 0 <= n < NGT:
                    mask(n)
                if batch_at(n, 0) == B - 1:
                    layer_norm(ln_index(1, B - 1), B - 1)
                if n == NGT - 4:
                    layer_norm(ln_index(2, 0), 0)
                if n == NGT - 2:
                    layer_norm(ln_index(2, 1), 1)
                if (b := batch_at(n, 1)) is not None:
                    low_qk(b, 0)
                if (b := batch_at(n, 2)) is not None:
                    low_qk(b, 1)
            route(B)
            ffn(1)

        @block.scalar
        def _(ac):
            for t in (2, 3):
                ac.dma_start(X[:, t, :], x[0, t * P:(t + 1) * P, :]).then_inc(ld_x[0], 16)
            ac.dma_start(id_f[:, :], ident).then_inc(ld_c, 16)
            ac.dma_start(rt_raw[:, :], router).then_inc(ld_w[0], 16)
            ac.dma_start(least_lead[:, :, :], least.partition_broadcast(P)).then_inc(ld_cf, 16)

            def high_weights(k):
                ac.wait_ge(ld_w[k], 16 * (1, 1, 1, 2, 3)[k])
                if k == 0:
                    nc.scalar.activation(rt_hi[:, :], rt_raw[:, :], ACT.Copy).then_inc(w_high, 1)
                else:
                    c = slice(*CUTS[k - 1])
                    nc.scalar.activation(w_hi[:, c], w_raw[:, c], ACT.Copy).then_inc(w_high, 1)

            def split_xt(n):
                ac.wait_ge(xt_ready, n + 1)
                nc.scalar.activation(XH[:, n % 3, :], M0[:, :], ACT.Copy).then_inc(xh_ready, 1)

            def silu(i):
                j, n = divmod(i, C)
                ac.wait_ge(h_ready, HID * j + n + 1)
                if i >= 3:
                    ac.wait_ge(y_ready, i - 2)
                nc.scalar.activation(act[:, i % 3, :], H_BANK[(HID * j + n) % 3][:, :], ACT.Silu).then_inc(act_ready, 1)

            def router_silu(j):
                ac.wait_ge(shift_ready, j + 1)
                if j >= 1:
                    ac.wait_ge(coef_ready, j)
                nc.scalar.activation(th[:, :], M1[:, 0:10 * NT].rearrange("p (t e) -> p t e", e=10)[:, :, E],
                                     ACT.Tanh, scale=0.5).then_inc(ex_ready, 1)
                nc.scalar.activation(sl[:, :, :], shifted[:, :, :], ACT.Silu).then_inc(ex_ready, 1)

            def ffn(kind):
                for b in range(B):
                    j = B * kind + b
                    for n in range(C):
                        silu(C * j + n)
                        if b + 1 < B:
                            if n == 1 and j != B:
                                split_xt(ln_index(2 * kind, b + 1))
                            if n == 3:
                                router_silu(j + 1)
                        if j == B - 3 and n == 5:
                            high_weights(4)
                        if (j, n) in PROJECT_ACT:
                            part, *of = PROJECT_ACT[j, n]
                            part(*of)
                        if n == 3 and j == B:
                            copy_at(B - 1)

            def high_qk(b, i):
                ac.wait_ge(qk_ready, 2 * b + i + 1)
                if b >= 1:
                    ac.wait_ge((scr_q, scr_k)[i], 48 * b)
                nc.scalar.activation(qk_parts[:, i, 0, :], MISC[:, :], ACT.Copy, scale=QK_SCALE[i]).then_inc(qk_high, 1)

            def middle_qk(b, i):
                ac.wait_ge(qk_sub, 2 * b + i + 1)
                nc.scalar.activation(qk_parts[:, i, 1, :], qk_rest[:, i, :], ACT.Copy).then_inc(mid_qk, 1)

            def values(b):
                ac.wait_ge(v_ready, b + 1)
                ac.wait_ge(va_set, 2)
                if b >= 2:
                    ac.wait_ge(pv_ready, NG * (b - 1))
                nc.scalar.activation(VA[b % 2][:, :, :, 0:HD],
                                     M0[:, :].rearrange("p (t h d) -> p t h d", t=NT, d=HD), ACT.Copy).then_inc(v_sb, 1)

            def exps(G, i):
                u = NU * G + i
                ac.wait_ge(t_ready, u + 1)
                if i == 0 and G >= 2:
                    ac.wait_ge(pv_ready, G - 1)
                a = prob_units(G % NG)[i]
                head = a[0][1] - GH * (G % NG)
                bank = T_BANK[u % 3]
                if a[0][2] == 2:
                    dst = probs[G % 2][:, head:head + 3:2, POS[2]:POS[2] + 2 * P]
                    src = bank[:, :].rearrange("p (h n) -> p h n", h=2)
                else:
                    pos = POS[a[0][2]]
                    dst, src = probs[G % 2][:, head, pos:pos + S], bank[:, :]
                nc.scalar.activation(dst, src, ACT.Exp).then_inc(exp_done, 1)

            def copy_nmax(G):
                ac.wait_ge(nmt_ready, G + 1)
                if G >= 2:
                    ac.wait_ge(nm_rows[G % 2], 64 * (G // 2))
                nc.scalar.activation(nmaxT[:, G % 2, :], MISC[0:GH * PARTS, 0:S // 2].bitcast(bf16), ACT.Copy).then_inc(nmt_sb, 1)

            def copy_out(G):
                ac.wait_ge(pv_ready, G + 1)
                if G >= 1:
                    ac.wait_ge(ott_ready, G)
                nc.scalar.activation(OT[:, :], O_BANK[:, :], ACT.Copy).then_inc(ot_sb, 1)

            def copy_at(b):
                ac.wait_ge(aot_ready, b + 1)
                if b >= 1:
                    ac.wait_ge(wo_ready, b)
                nc.scalar.activation(AT[:, :], M0[:, :], ACT.Copy).then_inc(at_sb, 1)

            PROJECT_ACT = {(2, 5): (split_xt, ln_index(1, 0)), (2, 7): (high_qk, 0, 0), (2, 8): (middle_qk, 0, 0),
                           (3, 0): (high_qk, 0, 1), (3, 1): (middle_qk, 0, 1), (3, 2): (values, 0),
                           (3, 3): (split_xt, ln_index(1, 1)), (3, 4): (high_qk, 1, 0), (3, 5): (middle_qk, 1, 0),
                           (3, 6): (high_qk, 1, 1), (3, 7): (middle_qk, 1, 1), (3, 8): (values, 1)}

            def load_table(k, function):
                nc.scalar.activation(table[:, k:k + 1], rt_raw[:, 0:1], function)

            ac.wait_ge(ld_w[0], 16)
            load_table(0, ACT.Silu)
            for k in range(2):
                high_weights(k)
            split_xt(0)
            for k in range(2, 4):
                high_weights(k)
            router_silu(0)
            ffn(0)
            load_table(1, ACT.Exp)
            for n in STEPS:
                for i in range(NU):
                    if 0 <= n < NGT:
                        exps(n, i)
                    if i == 3 and 0 <= n + 1 < NGT:
                        copy_nmax(n + 1)
                    if (b := batch_at(n, 1)) is not None:
                        if i == 5:
                            split_xt(ln_index(1, b))
                        if i == 8:
                            high_qk(b, 0)
                        if i == 9:
                            middle_qk(b, 0)
                    if (b := batch_at(n, 2)) is not None:
                        if i == 5:
                            high_qk(b, 1)
                        if i == 7:
                            middle_qk(b, 1)
                    if (b := batch_at(n, 3)) is not None and i == 9:
                        values(b)
                    if (b := batch_done(n)) is not None and i == 6:
                        copy_at(b)
                    if n == NGT - 2 and i == 5:
                        split_xt(ln_index(2, 0))
                    if n == NGT - 1 and i == 5:
                        split_xt(ln_index(2, 1))
                    if n == NGT and i == 0:
                        router_silu(B)
                if 0 <= n - 1 < NGT:
                    copy_out(n - 1)
            ffn(1)

        @block.vector
        def _(v):
            count = [0]

            def link(ins):
                count[0] += 1
                ins.then_inc(dve_chain, 1)
                v.wait_ge(dve_chain, count[0])

            def moments(kind, b):
                n = ln_index(kind, b)
                if n >= 1:
                    v.wait_ge(xn_ready, n)
                if kind == 0:
                    v.wait_ge(ld_x[b], 64 if b == 0 else 16)
                elif kind == 1:
                    v.wait_ge(y_used, C * (b + 1))
                else:
                    v.wait_ge(x_att, b + 1)
                for t in range(NT):
                    i = nc.vector.bn_stats(stats[:, t, :], X[:, b * NT + t, :])
                link(i)
                for t in range(NT):
                    i = nc.vector.bn_aggr(mv[:, t, :], stats[:, t, :])
                i.then_inc(mv_ready, 1)

            def split_xt(n):
                v.wait_ge(xh_ready, n + 1)
                nc.vector.tensor_tensor(XL[:, n % 3, :], M0[:, :], XH[:, n % 3, :], ALU.subtract).then_inc(xl_ready, 1)

            lg = M1[:, 0:10 * NT].rearrange("p (t e) -> p t e", e=10)

            def router_shift(j):
                v.wait_ge(lg_ready, j + 1)
                link(nc.vector.tensor_reduce(nmx[:, :], lg[:, :, 0:E], AX.X, ALU.max, negate=True))
                nc.vector.scalar_tensor_tensor(shifted[:, :, :], lg[:, :, 0:E], -1.0,
                                        nmx[:, :].unsqueeze(2).broadcast_to([P, NT, E]), ALU.add, ALU.add).then_inc(shift_ready, 1)

            def route_exp(j):
                v.wait_ge(ex_ready, 2 * (j + 1))
                if j >= 1:
                    v.wait_ge(coef_ready, j)
                link(nc.vector.tensor_tensor(rest[:, :, :], shifted[:, :, :], sl[:, :, :], ALU.subtract))
                link(nc.vector.reciprocal(rest[:, :, :], rest[:, :, :]))
                link(nc.vector.tensor_tensor(ex[:, :, :], sl[:, :, :], rest[:, :, :], ALU.mult))
                link(nc.vector.tensor_reduce(ssum[:, :], ex[:, :, :], AX.X, ALU.add))
                nc.vector.reciprocal(rsum[:, :], ssum[:, :]).then_inc(sm_ready, 1)

            def route_above(j):
                if j == 0:
                    v.wait_ge(ld_cf, 16)
                v.wait_ge(lead_ready, j + 1)
                nc.vector.tensor_tensor(above[:, :, :, :], lead[:, :, :, :],
                                        least_lead[:, :, :].unsqueeze(1).broadcast_to([P, NT, E, E]),
                                        ALU.is_gt).then_inc(above_ready, 1)

            def gate_up(j):
                i = C * j + E
                v.wait_ge(act_ready, i + 1)
                v.wait_ge(h_ready, HID * (j + 1))
                if j >= 1:
                    v.wait_ge(y_ready, C * j)
                nc.vector.tensor_tensor(gated[:, :], act[:, i % 3, :], H_BANK[(HID * j + E + 1) % 3][:, :],
                                        ALU.mult).then_inc(up_used, 1)

            def accumulate(i):
                j, n = divmod(i, C)
                b = j % B
                v.wait_ge(y_ready, i + 1)
                if n == 0:
                    v.wait_ge(coef_ready, j + 1)
                    if j >= B:
                        v.wait_ge(x_att, b + 1)
                if i >= 1:
                    v.wait_ge(y_used, i)
                for t in range(NT):
                    m = nc.vector.scalar_tensor_tensor(X[:, b * NT + t, :], Y_BANK[i % 3][:, t * P:(t + 1) * P],
                                                       coef[:, j % 2, t, n:n + 1], X[:, b * NT + t, :], ALU.mult, ALU.add)
                m.then_inc(y_used, 1)

            def ffn(kind):
                for b in range(B):
                    j = B * kind + b
                    for n in range(C):
                        if n == C - 2:
                            gate_up(j)
                        accumulate(C * j + n)
                        if b + 1 < B:
                            if n == 0 and j != B:
                                split_xt(ln_index(2 * kind, b + 1))
                            if n == 2:
                                router_shift(j + 1)
                            if n == 3:
                                route_exp(j + 1)
                            if n == 5:
                                route_above(j + 1)
                        if n == 6 and j == B - 3:
                            low_weights(4)
                        if j == B and n == 0:
                            normalise(NGT - 1)
                        if j == B and n == 5:
                            add_attention(B - 1)
                        if (j, n) in PROJECT_DVE:
                            part, *of = PROJECT_DVE[j, n]
                            part(*of)
                        before, after = LATER[kind][b]
                        if before and n == 1:
                            moments(*before)
                        if after and n == (8 if before else 6):
                            moments(*after)

            def rest_qk(b, i):
                v.wait_ge(qk_high, 2 * b + i + 1)
                if b >= 1:
                    v.wait_ge(parts_ready, 2 * (b - 1) + i + 1)
                nc.vector.scalar_tensor_tensor(qk_rest[:, i, :], MISC[:, :], QK_SCALE[i], qk_parts[:, i, 0, :],
                                               ALU.mult, ALU.subtract).then_inc(qk_sub, 1)

            def low_weights(k):
                v.wait_ge(w_high, k + 1)
                raw, hi, lo = (rt_raw, rt_hi, rt_lo) if k == 0 else (w_raw, w_hi, w_lo)
                c = slice(*CUTS[k - 1]) if k else slice(0, 10)
                nc.vector.tensor_tensor(lo[:, c], raw[:, c], hi[:, c], ALU.subtract).then_inc(w_split, 1)

            def maxima(G, i):
                u = NU * G + i
                v.wait_ge(s_ready, u + 1)
                a = score_units(G % NG)[i]
                bank = S_BANK[u % 3]
                hh = a[0][1] - GH * (G % NG)
                dst = nmax[:, G % 2]
                if a[0][2] == 1:
                    r = nc.vector.tensor_reduce(dst[:, hh:hh + 3:2, 1], bank[:, :].rearrange("p (h n) -> p h n", h=2),
                                                AX.X, ALU.max, negate=True)
                else:
                    for off, _, qt in a:
                        r = nc.vector.tensor_reduce(dst[:, hh, qt:qt + 1], bank[:, off:off + (qt + 1) * P],
                                                    AX.X, ALU.max, negate=True)
                r.then_inc(s_used, 1)

            def split_nmax(G):
                v.wait_ge(s_used, NU * (G + 1))
                if G >= 1:
                    v.wait_ge(nmt_ready, G)
                m = nmax[:, G % 2].rearrange("p h t -> p t h")
                r = nmax_rest[:, :, :].rearrange("p h t -> p t h")
                link(nc.vector.tensor_copy(nmax3[:, :, :, 0], m))
                link(nc.vector.tensor_tensor(r, m, nmax3[:, :, :, 0], ALU.subtract))
                link(nc.vector.tensor_copy(nmax3[:, :, :, 1], r))
                nc.vector.tensor_tensor(nmax3[:, :, :, 2], r, nmax3[:, :, :, 1], ALU.subtract).then_inc(nm3_ready, 1)

            def normalise(G):
                g = G % NG
                v.wait_ge(ott_ready, G + 1)
                o = MISC[:, :].rearrange("p (t h c) -> p t h c", t=NT, h=GH)
                link(nc.vector.reciprocal(rden[:, :, :], o[:, :, :, HD]))
                if g == 0 and G >= NG:
                    v.wait_ge(aot_ready, G // NG)
                dst = AO[:, :, GH * HD * g:GH * HD * (g + 1)].rearrange("p t (h d) -> p t h d", d=HD)
                i = nc.vector.tensor_tensor(dst, o[:, :, :, 0:HD], rden[:, :, :].unsqueeze(3).broadcast_to([P, NT, GH, HD]),
                                            ALU.mult)
                i.then_inc(ott_used, 1)

            def add_attention(b):
                v.wait_ge(wo_ready, b + 1)
                xt = X[:, b * NT:(b + 1) * NT, :]
                nc.vector.tensor_tensor(xt, xt, M0[:, :].rearrange("p (t d) -> p t d", t=NT), ALU.add).then_inc(x_att, 1)

            PROJECT_DVE = {(2, 4): (split_xt, ln_index(1, 0)), (2, 6): (rest_qk, 0, 0), (2, 8): (rest_qk, 0, 1),
                           (3, 2): (split_xt, ln_index(1, 1)), (3, 3): (rest_qk, 1, 0), (3, 5): (rest_qk, 1, 1)}

            moments(0, 0)
            v.wait_ge(mv_ready, 1)
            rsqrt(nc.vector, link)
            for t in range(NT):
                i = nc.vector.tensor_scalar(XN[:, 0, t, :], X[:, t, :], mv[:, t, 0:1], rstd[:, t:t + 1],
                                            ALU.subtract, ALU.mult)
            i.then_inc(xn_ready, 1)
            moments(0, 1)
            low_weights(0)
            split_xt(0)
            low_weights(1)
            low_weights(2)
            router_shift(0)
            low_weights(3)
            route_exp(0)
            route_above(0)
            ffn(0)
            for n in STEPS:
                for i in range(NU):
                    if 0 <= n + 2 < NGT:
                        maxima(n + 2, i)
                    if i == 1 and 0 <= n - 2 < NGT:
                        normalise(n - 2)
                    if batch_at(n, 0) == B - 1 and i == 6:
                        moments(1, B - 1)
                    if (b := batch_at(n, 1)) is not None:
                        if i == 5:
                            split_xt(ln_index(1, b))
                        if i == 8:
                            rest_qk(b, 0)
                    if (b := batch_at(n, 2)) is not None and i == 6:
                        rest_qk(b, 1)
                    if (b := batch_done(n)) is not None and i == 8:
                        add_attention(b)
                    if n == NGT - 4 and i == 6:
                        moments(2, 0)
                    if n == NGT - 2:
                        if i == 5:
                            split_xt(ln_index(2, 0))
                        if i == 6:
                            moments(2, 1)
                        if i == 8:
                            router_shift(B)
                    if n == NGT - 1 and i == 5:
                        split_xt(ln_index(2, 1))
                    if n == NGT and i == 2:
                        route_exp(B)
                    if n == NGT and i == 3:
                        route_above(B)
                if 0 <= n + 2 < NGT:
                    split_nmax(n + 2)
            ffn(1)

        @block.tensor
        def _(pe):
            def three_pass(dst, w_h, w_l, m_h, m_l):
                nc.tensor.matmul(dst, w_h, m_h, start=True, stop=False)
                nc.tensor.matmul(dst, w_h, m_l, start=False, stop=False)
                return nc.tensor.matmul(dst, w_l, m_h, start=False, stop=True)

            last_use = [None]

            def take_misc(used, value):
                if last_use[0]:
                    pe.wait_ge(*last_use[0])
                last_use[0] = (used, value)

            def transpose_xn(n, used, value):
                pe.wait_ge(xn_ready, n + 1)
                take_misc(used, value)
                for t in range(NT):
                    i = nc.tensor.transpose(M0[:, t * P:(t + 1) * P], XN[:, n % 2, t, :], id_f[:, :])
                i.then_inc(xt_ready, 1)

            def logits(j, n):
                pe.wait_ge(xl_ready, n + 1)
                if j >= 1:
                    pe.wait_ge(ex_ready, 2 * j)
                for t in range(NT):
                    c = slice(t * P, (t + 1) * P)
                    i = three_pass(M1[:, 10 * t:10 * t + 10], XH[:, n % 3, c], XL[:, n % 3, c], rt_hi[:, :], rt_lo[:, :])
                i.then_inc(lg_ready, 1)

            def hidden(j, n):
                i = HID * j + n
                ln = ln_index(2 * (j // B), j % B)
                if n == 0:
                    pe.wait_ge(xl_ready, ln + 1)
                if j == 0 and n in (0, 2, 6):
                    pe.wait_ge(w_split, {0: 2, 2: 3, 6: 4}[n])
                if i >= 3:
                    jj, nn = divmod(i - 3, HID)
                    if nn == E + 1:
                        pe.wait_ge(up_used, jj + 1)
                    else:
                        pe.wait_ge(act_ready, C * jj + nn + 1)
                c = slice(n * F, (n + 1) * F)
                three_pass(H_BANK[i % 3][:, :], w_hi[:, c], w_lo[:, c], XH[:, ln % 3, :], XL[:, ln % 3, :]).then_inc(h_ready, 1)

            def combine(j, n):
                i = C * j + n
                if n == E:
                    pe.wait_ge(up_used, j + 1)
                else:
                    pe.wait_ge(act_ready, i + 1)
                if i >= 3:
                    pe.wait_ge(y_used, i - 2)
                if j == 0 and n == 0:
                    pe.wait_ge(ld_w2, 32)
                for t in range(NT):
                    r = slice(t * P, (t + 1) * P)
                    a = gated[:, r] if n == E else act[:, i % 3, r]
                    m = nc.tensor.matmul(Y_BANK[i % 3][:, r], a, w2_sb[:, n, :], start=True, stop=True)
                m.then_inc(y_ready, 1)

            def ffn(kind):
                for b in range(B):
                    j, ln = B * kind + b, ln_index(2 * kind, b)
                    if b == 0:
                        hidden(j, 0)
                        hidden(j, 1)
                    for n in range(C):
                        if n + 2 < HID:
                            hidden(j, n + 2)
                        elif b + 1 < B:
                            hidden(j + 1, 0)
                            hidden(j + 1, 1)
                        combine(j, n)
                        if b + 1 < B:
                            if n == 0 and j != B:
                                transpose_xn(ln + 1, xl_ready, ln + 2)
                            if n == 2:
                                logits(j + 1, ln + 1)
                        if (j, n) in PROJECT_PE:
                            if (j, n) == (2, 6):
                                pe.wait_ge(w_split, 5)
                            part, *of = PROJECT_PE[j, n]
                            part(*of)
                        if j == B:
                            if n == 0:
                                transpose_out(NGT - 1)
                            if n == 2:
                                transpose_ao(B - 1)
                            if n == 4:
                                output(B - 1)

            def project(b, i):
                ln = ln_index(1, b)
                pe.wait_ge(xl_ready, ln + 1)
                take_misc(qk_sub, 2 * b + i + 1)
                c = slice((E + 2) * F + i * D, (E + 2) * F + (i + 1) * D)
                three_pass(MISC[:, :], w_hi[:, c], w_lo[:, c], XH[:, ln % 3, :], XL[:, ln % 3, :]).then_inc(qk_ready, 1)

            def values(b):
                ln = ln_index(1, b)
                c = slice((E + 2) * F + 2 * D, (E + 2) * F + 3 * D)
                take_misc(v_sb, b + 1)
                for t in range(NT):
                    r = slice(t * P, (t + 1) * P)
                    m = three_pass(MISC[:, r], XH[:, ln % 3, r], XL[:, ln % 3, r], w_hi[:, c], w_lo[:, c])
                m.then_inc(v_ready, 1)

            def scores(G, i):
                b, g = divmod(G, NG)
                u = NU * G + i
                if u >= 3:
                    pe.wait_ge(s_used, u - 2)
                if i == 0 and g == 0:
                    pe.wait_ge(qa_ready[b % 2], 32 * (b // 2 + 1))
                    pe.wait_ge(ka_ready[b % 2], 32 * (b // 2 + 1))
                for off, h, qt in score_units(g)[i]:
                    lo = 64 * (h % 2)
                    r = slice(lo, lo + ROWS_S)
                    dst = S_BANK[u % 3]
                    n = (qt + 1) * P
                    nc.tensor.matmul(dst[:, off:off + n], QA[b % 2][r, h // 2, qt * P:(qt + 1) * P],
                                     KA[b % 2][r, h // 2, 0:n], start=True, stop=False, skip_group_check=True)
                    m = nc.tensor.matmul(dst[:, off + qt * P:off + n], id_b[:, :], causal_sb[:, :],
                                         start=False, stop=True, skip_group_check=True)
                m.then_inc(s_ready, 1)

            def transpose_nmax(G):
                pe.wait_ge(nm3_ready, G + 1)
                take_misc(nmt_sb, G + 1)
                dst = MISC[0:GH * PARTS, 0:S // 2].bitcast(bf16)
                for t in range(NT):
                    i = nc.tensor.transpose(dst[:, t * P:(t + 1) * P], nmax3[:, t, :, :].rearrange("p h a -> p (h a)"), id_b[:, :])
                i.then_inc(nmt_ready, 1)

            def scores_t(G, i):
                b, g = divmod(G, NG)
                u = NU * G + i
                if i == 0:
                    pe.wait_ge(nm_rows[G % 2], 64 * (G // 2 + 1))
                if u >= 3:
                    pe.wait_ge(exp_done, u - 2)
                for off, h, kt in prob_units(g)[i]:
                    lo = 64 * (h % 2)
                    r = slice(lo, lo + ROWS_T)
                    m = nc.tensor.matmul(T_BANK[u % 3][:, off:off + WID[kt]], KA[b % 2][r, h // 2, kt * P:(kt + 1) * P],
                                         QA[b % 2][r, h // 2, kt * P:S], start=True, stop=True, skip_group_check=True)
                m.then_inc(t_ready, 1)

            PIECES = ((0, 0, 256), (0, 256, 512), (3, 384, 512), (1, 128, 512), (2, 256, 512))
            PIECE_SLOTS = (2, 3, 5, 6, 8)

            def weigh_values(G, k):
                b, g = divmod(G, NG)
                kt, q0, q1 = PIECES[k]
                pe.wait_ge(masked, NT * G + {0: 1, 3: 2, 1: 3, 2: 4}[kt])
                if k == 0:
                    if G >= 1:
                        pe.wait_ge(ot_sb, G)
                    if g == 0:
                        pe.wait_ge(v_sb, b + 1)
                at = POS[kt] - kt * P
                for hh in range(GH):
                    m = nc.tensor.matmul(O_BANK[32 * hh:32 * hh + 32, q0:q1], VA[b % 2][:, kt, GH * g + hh, :],
                                         probs[G % 2][:, hh, at + q0:at + q1],
                                         start=(k == 0), stop=(k == len(PIECES) - 1), skip_group_check=True)
                if k == len(PIECES) - 1:
                    m.then_inc(pv_ready, 1)

            def transpose_out(G):
                pe.wait_ge(ot_sb, G + 1)
                take_misc(ott_used, G + 1)
                for t in range(NT):
                    i = nc.tensor.transpose(MISC[:, t * P:(t + 1) * P], OT[:, t * P:(t + 1) * P], id_f[:, :])
                i.then_inc(ott_ready, 1)

            def transpose_ao(b):
                pe.wait_ge(ott_used, NG * (b + 1))
                take_misc(at_sb, b + 1)
                for t in range(NT):
                    i = nc.tensor.transpose(MISC[:, t * P:(t + 1) * P], AO[:, t, :], id_f[:, :])
                i.then_inc(aot_ready, 1)

            def output(b):
                take_misc(x_att, b + 1)
                for t in range(NT):
                    m = nc.tensor.matmul(MISC[:, t * P:(t + 1) * P], AT[:, t * P:(t + 1) * P], wo_sb[:, :], start=True, stop=True)
                m.then_inc(wo_ready, 1)

            ln0, ln1 = ln_index(1, 0), ln_index(1, 1)
            PROJECT_PE = {(2, 4): (transpose_xn, ln0, xl_ready, ln0 + 1), (2, 6): (project, 0, 0), (2, 8): (project, 0, 1),
                          (3, 0): (values, 0), (3, 2): (transpose_xn, ln1, xl_ready, ln1 + 1),
                          (3, 3): (project, 1, 0), (3, 5): (project, 1, 1), (3, 7): (values, 1)}

            pe.wait_ge(ld_c, 16)
            transpose_xn(0, xl_ready, 1)
            pe.wait_ge(w_split, 1)
            logits(0, 0)
            ffn(0)
            pe.wait_ge(up_used, B)
            pe.wait_ge(ld_ac, 16 * 11)
            for n in STEPS:
                for i in range(NU):
                    if n == 0 and i == 0:
                        pe.wait_ge(y_used, C * B)
                    if 0 <= n < NGT:
                        scores_t(n, i)
                    if 0 <= n + 2 < NGT:
                        scores(n + 2, i)
                    if i == 1 and 0 <= n - 2 < NGT:
                        transpose_out(n - 2)
                    if i == 3 and 0 <= n + 1 < NGT:
                        transpose_nmax(n + 1)
                    if i in PIECE_SLOTS and 0 <= n - 1 < NGT:
                        weigh_values(n - 1, PIECE_SLOTS.index(i))
                    if (b := batch_at(n, 1)) is not None:
                        if i == 5:
                            transpose_xn(ln_index(1, b), xl_ready, ln_index(1, b) + 1)
                        if i == 8:
                            project(b, 0)
                    if (b := batch_at(n, 2)) is not None and i == 5:
                        project(b, 1)
                    if (b := batch_at(n, 3)) is not None and i == 8:
                        values(b)
                    if (b := batch_done(n)) is not None:
                        if i == 5:
                            transpose_ao(b)
                        if i == 7:
                            output(b)
                    if n == NGT - 2:
                        if i == 4:
                            transpose_xn(ln_index(2, 0), xl_ready, ln_index(2, 0) + 1)
                        if i == 7:
                            pe.wait_ge(s_used, NU * NGT)
                            logits(B, ln_index(2, 0))
                    if n == NGT - 1 and i == 5:
                        transpose_xn(ln_index(2, 1), xl_ready, ln_index(2, 1) + 1)
            pe.wait_ge(exp_done, NU * NGT)
            pe.wait_ge(ot_sb, NGT)
            ffn(1)


def kernel(**inputs):
    import numpy as np
    import ml_dtypes
    import concourse.bacc as bacc
    from concourse import mybir
    from concourse.bass_utils import run_bass_kernel_spmd as run

    bf = ml_dtypes.bfloat16
    H, S, E, P = 16, 512, 8, 128
    slopes = np.array([1.0 / ((2.0 ** 8) ** (1.0 / H)) ** (i + 1) for i in range(H)], np.float32)

    def parts(a):
        out, rest = [], np.asarray(a, np.float64)
        for _ in range(3):
            out.append(rest.astype(np.float32).astype(bf))
            rest = rest - out[-1].astype(np.float64)
        return out

    lift = slopes.astype(np.float64)[:, None] * np.arange(S)
    ones = [np.ones((H, S), bf)]
    by_pair = lambda rows: np.ascontiguousarray(np.stack(rows).reshape(len(rows), H // 2, 2, S).transpose(2, 0, 1, 3))
    a = {k: np.asarray(v) for k, v in inputs.items()}
    arrays = {
        "x": a["L0_attn_x"],
        "w1": a["L0_ffn_w1"],
        "w2": a["L0_ffn_w2"],
        "gate_up": a["L0_ffn_shared_gate_up"],
        "down": a["L0_ffn_shared_down"],
        "router": np.concatenate([a["L0_ffn_router_w"], a["L0_ffn_shared_gate_w"], np.zeros((P, 1), np.float32)], 1),
        "wq": a["L0_attn_Wq"].T, "wk": a["L0_attn_Wk"].T, "wv": a["L0_attn_Wv"].T, "wo": a["L0_attn_Wo"].T,
        "q_const": by_pair(ones * 3 + parts(lift)),
        "k_const": by_pair(parts(-lift) + ones * 6),
        "least": np.tril(np.full((E, E), -1.2e-38, np.float32), -1),
        "causal": np.triu(np.full((P, P), -1e30, np.float32), 1).astype(bf),
        "ident": np.eye(P, dtype=np.float32),
        "ident_b": np.eye(P, dtype=np.float32).astype(bf),
    }
    nc = bacc.Bacc("TRN2", target_bir_lowering=False, num_devices=1)
    data, args = {}, []
    for name, v in arrays.items():
        v = np.ascontiguousarray(v)
        data["in_" + name] = v
        args.append(nc.dram_tensor("in_" + name, v.shape, mybir.dt.from_np(v.dtype), kind="ExternalInput").ap())
    args.append(nc.dram_tensor("out_x", a["L0_attn_x"].shape, mybir.dt.float32, kind="ExternalOutput").ap())
    macaron_block(nc, *args)
    r = run(nc, [data], core_ids=[0])
    return r.results[0]["out_x"]
```

```python
import concourse.bass as bass
from concourse import mybir
from contextlib import ExitStack


def macaron_block(nc: bass.Bass, x, w1, w2, gate_up, down, router, wq, wk, wv, wo,
                  q_const, k_const, least, causal, ident, ident_b, out):
    f32, f32r, bf16 = mybir.dt.float32, mybir.dt.float32r, mybir.dt.bfloat16
    i32 = mybir.dt.int32
    ALU, ACT, AX = mybir.AluOpType, mybir.ActivationFunctionType, mybir.AxisListType

    P = 128
    B, S, D = x.shape
    E, _, F = w1.shape
    NT = S // P
    H, HD = 16, D // 16
    NP = H // 2
    GH = 4
    NG = H // GH
    C = E + 1
    PARTS = 3
    PROD = 6 * HD
    ROWS_S, ROWS_T = PROD + 6, PROD + 9
    VW = 32
    RW = 10
    EPS = 1e-5
    RSQRT_MAGIC = float(0x5F3759DF)
    SPAN = P * (NT * (NT + 1) // 2)
    WID = [S - P * kt for kt in range(NT)]

    ctx = ExitStack()
    with ctx:
        def sb(name, shape, dt=f32):
            return ctx.enter_context(nc.sbuf_tensor(name, shape, dt))

        def sem(name):
            return ctx.enter_context(nc.semaphore(name))

        NW = E * F + 2 * F + 3 * D
        w_raw = sb("w_raw", [P, NW])
        w_hi, w_lo = sb("w_hi", [P, NW], f32r), sb("w_lo", [P, NW], f32r)
        rt_raw, rt_parts = sb("rt_raw", [P, RW]), sb("rt_parts", [P, 2 * RW], f32r)
        w2_sb = sb("w2_sb", [P, C, D])
        wo_sb = sb("wo_sb", [P, D])
        id_f, id_b = sb("id_f", [P, P]), sb("id_b", [P, P], bf16)
        least_lead = sb("least_lead", [P, E, E])
        causal_sb = sb("causal_sb", [P, P], bf16)
        X = sb("X", [P, B * NT, D])
        stats, mv, rstd = sb("stats", [P, NT, 6]), sb("mv", [P, NT, 2]), sb("rstd", [P, NT])
        vhalf, newton = sb("vhalf", [P, NT]), sb("newton", [P, NT])
        XN = sb("XN", [P, 2, NT, D])
        XH, XL = sb("XH", [P, 3, S], f32r), sb("XL", [P, 3, S], f32r)
        table = sb("table", [P, 3])
        nmx, shifted, ex = sb("nmx", [P, NT]), sb("shifted", [P, NT, E]), sb("ex", [P, NT, E])
        sl = sb("sl", [P, NT, E])
        th, ssum, rsum = sb("th", [P, NT]), sb("ssum", [P, NT]), sb("rsum", [P, NT])
        above, lead = sb("above", [P, NT, E, E]), sb("lead", [P, NT, E, E])
        low, lg = sb("low", [P, NT, C]), sb("lg", [P, NT, C])
        kept, coef = sb("kept", [P, NT, E]), sb("coef", [P, 2, NT, C])
        rest = sb("rest", [P, NT, E])
        act = sb("act", [P, 3, S])
        gated = sb("gated", [P, S])
        qk_rest = sb("qk_rest", [P, 2, S])
        qk_parts = sb("qk_parts", [P, 2, 2, PARTS, S], bf16)
        QA = [sb(f"QA{i}", [P, NP, S], bf16) for i in range(2)]
        KA = [sb(f"KA{i}", [P, NP, S], bf16) for i in range(2)]
        VA = [sb(f"VA{i}", [P, NT, H, VW]) for i in range(2)]
        nmax = sb("nmax", [P, 2, GH, NT])
        nmax_rest = sb("nmax_rest", [P, GH, NT])
        nmax3 = sb("nmax3", [P, NT, GH, PARTS], bf16)
        nmaxT = sb("nmaxT", [GH * PARTS, 2, S], bf16)
        probs = [sb(f"probs{i}", [P, GH, SPAN]) for i in range(2)]
        OT = sb("OT", [P, S])
        rden = sb("rden", [P, NT, GH])
        AO = sb("AO", [P, NT, D])
        AT = sb("AT", [P, S])
        scratch = nc.dram_tensor("qk_scratch", [2, B, P, 6, S], bf16, kind="Internal").ap()

        banks = [ctx.enter_context(nc.psum_tensor(f"bank{i}", [P, S], f32)) for i in range(8)]
        H_BANK, Y_BANK, M0, M1 = banks[0:3], banks[3:6], banks[6], banks[7]
        S_BANK, T_BANK, O_BANK, MISC = [banks[0], banks[1], banks[7]], banks[2:5], banks[5], banks[6]

        ld_x = [sem(f"ld_x{b}") for b in range(B)]
        ld_w = [sem(f"ld_weights{k}") for k in range(5)]
        ld_c, ld_cf, ld_w2, ld_ac = sem("ld_c"), sem("ld_cf"), sem("ld_w2"), sem("ld_ac")
        w_high, w_split = sem("w_high"), sem("w_split")
        va_set = sem("va_set")
        mv_ready = sem("mv_ready")
        xn_ready, xt_ready, xh_ready, xl_ready = sem("xn_ready"), sem("xt_ready"), sem("xh_ready"), sem("xl_ready")
        lg_ready, shift_ready, ex_ready = sem("lg_ready"), sem("shift_ready"), sem("ex_ready")
        sm_ready, lead_ready, above_ready = sem("sm_ready"), sem("lead_ready"), sem("above_ready")
        coef_ready = sem("coef_ready")
        h_ready, act_ready, up_used = sem("h_ready"), sem("act_ready"), sem("up_used")
        y_ready, y_used = sem("y_ready"), sem("y_used")
        qk_ready, qk_high, qk_sub = sem("qk_ready"), sem("qk_high"), sem("qk_sub")
        mid_qk, parts_ready = sem("mid_qk"), sem("parts_ready")
        v_ready, v_sb = sem("v_ready"), sem("v_sb")
        scr_q, scr_k = sem("scr_q"), sem("scr_k")
        qa_ready, ka_ready = [sem("qa_ready0"), sem("qa_ready1")], [sem("ka_ready0"), sem("ka_ready1")]
        aot_ready, at_sb, wo_ready, x_att = sem("aot_ready"), sem("at_sb"), sem("wo_ready"), sem("x_att")
        s_ready, s_used = sem("s_ready"), sem("s_used")
        nm3_ready, nmt_ready, nmt_sb = sem("nm3_ready"), sem("nmt_ready"), sem("nmt_sb")
        nm_rows = [sem("nm_rows0"), sem("nm_rows1")]
        t_ready, exp_done, masked = sem("t_ready"), sem("exp_done"), sem("masked")
        pv_ready, ot_sb, ott_ready, ott_used = sem("pv_ready"), sem("ot_sb"), sem("ott_ready"), sem("ott_used")
        stored = sem("stored")
        dve_chain, pool_chain = sem("dve_chain"), sem("pool_chain")

        block = ctx.enter_context(nc.Block())

        HID = E + 2
        LATER = (((0, 2), None), ((0, 3), (1, 0)), (None, (1, 1)), ((1, 2), None)), \
                (((2, 2), None), ((2, 3), None), (None, None), (None, None))
        CUTS = ((0, 2 * F), (2 * F, 6 * F), (6 * F, (E + 2) * F), ((E + 2) * F, NW))
        NU = 10

        def ln_index(kind, b):
            return kind * B + b

        def rsqrt(engine, link, fused):
            link(engine.tensor_scalar(vhalf[:, :], mv[:, :, 1], EPS, None, ALU.add))
            link(engine.tensor_scalar(rstd[:, :].bitcast(i32), vhalf[:, :].bitcast(i32), -0.5, RSQRT_MAGIC, ALU.mult, ALU.add))
            link(engine.tensor_scalar(vhalf[:, :], vhalf[:, :], -0.5, None, ALU.mult))
            for _ in range(3):
                link(engine.tensor_tensor(newton[:, :], rstd[:, :], vhalf[:, :], ALU.mult))
                link(engine.tensor_tensor(newton[:, :], newton[:, :], rstd[:, :], ALU.mult))
                if fused:
                    link(engine.scalar_tensor_tensor(rstd[:, :], newton[:, :], 1.5, rstd[:, :], ALU.add, ALU.mult))
                else:
                    link(engine.tensor_scalar(newton[:, :], newton[:, :], 1.5, None, ALU.add))
                    link(engine.tensor_tensor(rstd[:, :], newton[:, :], rstd[:, :], ALU.mult))

        def score_units(g):
            heads = range(GH * g, GH * g + GH)
            return ([[(0, h, 3)] for h in heads] + [[(0, h, 2), (3 * P, h, 0)] for h in heads]
                    + [[(0, h, 1), (2 * P, h + 2, 1)] for h in heads[:2]])

        def prob_units(g):
            heads = range(GH * g, GH * g + GH)
            return ([[(0, h, 0)] for h in heads] + [[(0, h, 3), (P, h, 1)] for h in heads]
                    + [[(0, h, 2), (2 * P, h + 2, 2)] for h in heads[:2]])

        POS = {0: 0, 3: 512, 1: 640, 2: 1024}
        NGT = B * NG

        STEPS = range(-2, NGT + 1)
        QK_SCALE = (float(HD) ** -0.5, 1.0)

        def batch_at(n, phase):
            b, rest = divmod(n + 7 - phase, NG)
            return b if rest == 0 and 2 <= b < B else None

        def projected_at(n, phase):
            if batch_at(n + NG, phase) == 2:
                return 2
            return b if (b := batch_at(n, phase)) != 2 else None

        OUT_SLOT = 7
        VALUE_SLOTS = ((-2, 2), (-2, 6))
        LAST_LN = 3
        XT_TAIL = ((NGT - 2, 4), (NGT - 1, 3))

        def batch_done(n):
            b, rest = divmod(n - 5, NG)
            return b if rest == 0 and 0 <= b < B else None

        @block.sync
        def _(sp):
            for t in (0, 1):
                sp.dma_start(X[:, t, :], x[0, t * P:(t + 1) * P, :]).then_inc(ld_x[0], 16)
            sp.dma_start(w_raw[:, 0:2 * F].rearrange("p (e f) -> p e f", f=F),
                         w1[0:2].rearrange("e d f -> d e f")).then_inc(ld_w[1], 16)
            sp.dma_start(w_raw[:, 2 * F:6 * F].rearrange("p (e f) -> p e f", f=F),
                         w1[2:6].rearrange("e d f -> d e f")).then_inc(ld_w[2], 16)
            sp.dma_start(w2_sb[:, 0:E, :], w2.rearrange("e f d -> f e d")).then_inc(ld_w2, 16)
            sp.dma_start(w_raw[:, 6 * F:E * F].rearrange("p (e f) -> p e f", f=F),
                         w1[6:E].rearrange("e d f -> d e f")).then_inc(ld_w[3], 16)
            sp.dma_start(w_raw[:, E * F:(E + 2) * F], gate_up).then_inc(ld_w[3], 16)
            sp.dma_start(w2_sb[:, E, :], down).then_inc(ld_w2, 16)
            for b in range(1, B):
                sp.dma_start(X[:, b * NT:(b + 1) * NT, :], x[b].rearrange("(t p) d -> p t d", p=P)).then_inc(ld_x[b], 16)
            for i, w in enumerate((wq, wk, wv)):
                sp.dma_start(w_raw[:, (E + 2) * F + i * D:(E + 2) * F + (i + 1) * D], w).then_inc(ld_w[4], 16)
            sp.dma_start(id_b[:, :], ident_b).then_inc(ld_ac, 16)
            sp.dma_start(wo_sb[:, :], wo).then_inc(ld_ac, 16)
            sp.dma_start(causal_sb[:, :], causal).then_inc(ld_ac, 16)
            for i in range(2):
                for par in range(2):
                    sp.dma_start(QA[i][64 * par + PROD:64 * par + PROD + 6, :, :], q_const[par]).then_inc(ld_ac, 16)
                    sp.dma_start(KA[i][64 * par + PROD:64 * par + PROD + 9, :, :], k_const[par]).then_inc(ld_ac, 16)

            def write_parts(b, i):
                sp.wait_ge(parts_ready, 2 * b + i + 1)
                part, dst = qk_parts[:, b % 2, i], scratch[i, b]
                if i == 0:
                    sp.dma_start(dst[:, 0:3, :], part[:, 0, :].unsqueeze(1).broadcast_to([P, 3, S])).then_inc(scr_q, 16)
                    sp.dma_start(dst[:, 3:5, :], part[:, 1, :].unsqueeze(1).broadcast_to([P, 2, S])).then_inc(scr_q, 16)
                    sp.dma_start(dst[:, 5, :], part[:, 2, :]).then_inc(scr_q, 16)
                else:
                    sp.dma_start(dst[:, 0:3, :], part[:, 0:3, :]).then_inc(scr_k, 16)
                    sp.dma_start(dst[:, 3:5, :], part[:, 0:2, :]).then_inc(scr_k, 16)
                    sp.dma_start(dst[:, 5, :], part[:, 0, :]).then_inc(scr_k, 16)

            def read_rows(b):
                if b >= 2:
                    sp.wait_ge(t_ready, NU * NG * (b - 1))
                for i, (scr, to, ready) in enumerate(((scr_q, QA, qa_ready), (scr_k, KA, ka_ready))):
                    sp.wait_ge(scr, 48 * (b + 1))
                    rows = scratch[i, b].rearrange("(pair par d) s n -> par d s pair n", par=2, d=HD)
                    for par in range(2):
                        sp.dma_start(to[b % 2][64 * par:64 * par + PROD, :, :],
                                     rows[par].rearrange("d s pair n -> (d s) pair n")).then_inc(ready[b % 2], 16)

            def maximum_rows(G):
                b, g = divmod(G, NG)
                sp.wait_ge(nmt_sb, G + 1)
                for hh in range(GH):
                    h = GH * g + hh
                    sp.dma_start(QA[b % 2][64 * (h % 2) + ROWS_S:64 * (h % 2) + ROWS_T, h // 2, :],
                                 nmaxT[PARTS * hh:PARTS * (hh + 1), G % 2, :]).then_inc(nm_rows[G % 2], 16)

            for b in range(2):
                write_parts(b, 0)
                write_parts(b, 1)
                read_rows(b)
            for n in STEPS:
                if (b := batch_at(n, 4)) is not None:
                    read_rows(b)
                if 0 <= n + 1 < NGT:
                    maximum_rows(n + 1)
                if (b := projected_at(n, 2)) is not None:
                    write_parts(b, 0)
                if (b := projected_at(n, 3)) is not None:
                    write_parts(b, 1)
            for b in range(B):
                sp.wait_ge(y_used, C * (B + b + 1))
                sp.dma_start(out[b].rearrange("(t p) d -> p t d", p=P), X[:, b * NT:(b + 1) * NT, :]).then_inc(stored, 16)
            sp.wait_ge(stored, 16 * B)

        @block.gpsimd
        def _(pool):
            count = [0]

            def link(ins):
                count[0] += 1
                ins.then_inc(pool_chain, 1)
                pool.wait_ge(pool_chain, count[0])

            def layer_norm(n, b):
                pool.wait_ge(mv_ready, n + 1)
                rsqrt(nc.gpsimd, link, False)
                if n >= 2:
                    pool.wait_ge(xt_ready, n - 1)
                link(nc.gpsimd.tensor_tensor(XN[:, n % 2], X[:, b * NT:(b + 1) * NT, :],
                                             mv[:, :, 0:1].broadcast_to([P, NT, D]), ALU.subtract))
                nc.gpsimd.tensor_tensor(XN[:, n % 2], XN[:, n % 2], rstd[:, :].unsqueeze(2).broadcast_to([P, NT, D]),
                                        ALU.mult).then_inc(xn_ready, 1)

            def route(j):
                pool.wait_ge(sm_ready, j + 1)
                other = ex[:, :, :].unsqueeze(2).broadcast_to([P, NT, E, E])
                own = ex[:, :, :].unsqueeze(3).broadcast_to([P, NT, E, E])
                nc.gpsimd.tensor_tensor(lead[:, :, :, :], other, own, ALU.subtract).then_inc(lead_ready, 1)
                pool.wait_ge(above_ready, j + 1)
                half = E // 2
                while half:
                    link(nc.gpsimd.tensor_tensor(above[:, :, :, 0:half], above[:, :, :, 0:half],
                                                 above[:, :, :, half:2 * half], ALU.add))
                    half //= 2
                link(nc.gpsimd.tensor_scalar(kept[:, :, :], above[:, :, :, 0], 1.5, 0.5, ALU.is_lt, ALU.mult))
                link(nc.gpsimd.tensor_tensor(kept[:, :, :], kept[:, :, :], ex[:, :, :], ALU.mult))
                if j >= 2:
                    pool.wait_ge(y_used, C * (j - 1))
                nc.gpsimd.tensor_scalar(coef[:, j % 2, :, E], th[:, :], 1.0, 0.25, ALU.add, ALU.mult)
                nc.gpsimd.tensor_tensor(coef[:, j % 2, :, 0:E], kept[:, :, :],
                                        rsum[:, :].unsqueeze(2).broadcast_to([P, NT, E]), ALU.mult).then_inc(coef_ready, 1)

            def ffn(kind):
                for b in range(B):
                    before, after = LATER[kind][b]
                    if kind == 0 and b == B - 1:
                        low_qk(0, 0)
                        low_qk(0, 1)
                    if before:
                        layer_norm(ln_index(*before), before[1])
                    if kind == 0 and b == B - 1:
                        low_qk(1, 0)
                        low_qk(1, 1)
                    if b + 1 < B:
                        route(B * kind + b + 1)
                    if after:
                        layer_norm(ln_index(*after), after[1])

            layer_norm(1, 1)
            route(0)
            for i in range(2):
                link(nc.gpsimd.memset(VA[i][:, :, :, :], 0.0))
            for i in range(2):
                nc.gpsimd.memset(VA[i][:, :, :, HD:HD + 1], 1.0).then_inc(va_set, 1)

            def low_qk(b, i):
                pool.wait_ge(mid_qk, 2 * b + i + 1)
                nc.gpsimd.tensor_tensor(qk_parts[:, b % 2, i, 2, :], qk_rest[:, i, :], qk_parts[:, b % 2, i, 1, :],
                                        ALU.subtract).then_inc(parts_ready, 1)

            def split_nmax(G):
                pool.wait_ge(s_used, NU * (G + 1))
                if G >= 1:
                    pool.wait_ge(nmt_ready, G)
                m = nmax[:, G % 2].rearrange("p h t -> p t h")
                r = nmax_rest[:, :, :].rearrange("p h t -> p t h")
                link(nc.gpsimd.tensor_copy(nmax3[:, :, :, 0], m))
                link(nc.gpsimd.tensor_tensor(r, m, nmax3[:, :, :, 0], ALU.subtract))
                link(nc.gpsimd.tensor_copy(nmax3[:, :, :, 1], r))
                nc.gpsimd.tensor_tensor(nmax3[:, :, :, 2], r, nmax3[:, :, :, 1], ALU.subtract).then_inc(nm3_ready, 1)

            def mask(G, tiles):
                for kt, need in tiles:
                    pool.wait_ge(exp_done, NU * G + need)
                    blk = probs[G % 2][:, :, POS[kt]:POS[kt] + P]
                    nc.gpsimd.affine_select(out=blk, in_=blk, compare_op=ALU.is_ge, fill=0.0, base=0,
                                            pattern=[[0, GH], [1, P]], channel_multiplier=-1).then_inc(masked, 1)

            ffn(0)
            for n in STEPS:
                if 0 <= n < NGT:
                    mask(n, ((0, 4), (3, 8), (1, 8)))
                for k in range(2):
                    if (b := projected_at(n, 2 + k)) is not None:
                        low_qk(b, k)
                if 0 <= n < NGT:
                    mask(n, ((2, 10),))
                if 0 <= n + 2 < NGT:
                    split_nmax(n + 2)
                if n == LAST_LN:
                    layer_norm(ln_index(1, B - 1), B - 1)
                if n == NGT - 6:
                    layer_norm(ln_index(2, 0), 0)
                if n == NGT - 4:
                    layer_norm(ln_index(2, 1), 1)
            route(B)
            ffn(1)

        @block.scalar
        def _(ac):
            for t in (2, 3):
                ac.dma_start(X[:, t, :], x[0, t * P:(t + 1) * P, :]).then_inc(ld_x[0], 16)
            ac.dma_start(id_f[:, :], ident).then_inc(ld_c, 16)
            ac.dma_start(rt_raw[:, :], router).then_inc(ld_w[0], 16)
            ac.dma_start(least_lead[:, :, :], least.partition_broadcast(P)).then_inc(ld_cf, 16)

            def high_weights(k):
                ac.wait_ge(ld_w[k], 16 * (1, 1, 1, 2, 3)[k])
                if k == 0:
                    nc.scalar.activation(rt_parts[:, 0:RW], rt_raw[:, :], ACT.Copy).then_inc(w_high, 1)
                else:
                    c = slice(*CUTS[k - 1])
                    nc.scalar.activation(w_hi[:, c], w_raw[:, c], ACT.Copy).then_inc(w_high, 1)

            def split_xt(n):
                ac.wait_ge(xt_ready, n + 1)
                nc.scalar.activation(XH[:, n % 3, :], M0[:, :], ACT.Copy).then_inc(xh_ready, 1)

            def silu(i):
                j, n = divmod(i, C)
                ac.wait_ge(h_ready, HID * j + n + 1)
                if i >= 3:
                    ac.wait_ge(y_ready, i - 2)
                nc.scalar.activation(act[:, i % 3, :], H_BANK[(HID * j + n) % 3][:, :], ACT.Silu).then_inc(act_ready, 1)

            def router_silu(j):
                ac.wait_ge(shift_ready, j + 1)
                if j >= 1:
                    ac.wait_ge(coef_ready, j)
                nc.scalar.activation(th[:, :], lg[:, :, E],
                                     ACT.Tanh, scale=0.5).then_inc(ex_ready, 1)
                nc.scalar.activation(sl[:, :, :], shifted[:, :, :], ACT.Silu).then_inc(ex_ready, 1)

            def ffn(kind):
                for b in range(B):
                    j = B * kind + b
                    for n in range(C):
                        if j != B or n > 1:
                            silu(C * j + n)
                        if b + 1 < B:
                            if n == 1 and j != B:
                                split_xt(ln_index(2 * kind, b + 1))
                            if n == 4:
                                router_silu(j + 1)
                        if j == B - 3 and n == 5:
                            high_weights(4)
                        if (j, n) in PROJECT_ACT:
                            part, *of = PROJECT_ACT[j, n]
                            part(*of)
                        if n == 3 and j == B:
                            copy_at(B - 1)

            def high_qk(b, i):
                ac.wait_ge(qk_ready, 2 * b + i + 1)
                if b >= 2:
                    ac.wait_ge((scr_q, scr_k)[i], 48 * (b - 1))
                nc.scalar.activation(qk_parts[:, b % 2, i, 0, :], MISC[:, :], ACT.Copy, scale=QK_SCALE[i]).then_inc(qk_high, 1)

            def middle_qk(b, i):
                ac.wait_ge(qk_sub, 2 * b + i + 1)
                nc.scalar.activation(qk_parts[:, b % 2, i, 1, :], qk_rest[:, i, :], ACT.Copy).then_inc(mid_qk, 1)

            def values(b):
                ac.wait_ge(v_ready, b + 1)
                ac.wait_ge(va_set, 2)
                if b >= 2:
                    ac.wait_ge(pv_ready, NG * (b - 1))
                nc.scalar.activation(VA[b % 2][:, :, :, 0:HD],
                                     M0[:, :].rearrange("p (t h d) -> p t h d", t=NT, d=HD), ACT.Copy).then_inc(v_sb, 1)

            def exps(G, i):
                u = NU * G + i
                ac.wait_ge(t_ready, u + 1)
                if i == 0 and G >= 2:
                    ac.wait_ge(pv_ready, G - 1)
                a = prob_units(G % NG)[i]
                head = a[0][1] - GH * (G % NG)
                bank = T_BANK[u % 3]
                if a[0][2] == 2:
                    dst = probs[G % 2][:, head:head + 3:2, POS[2]:POS[2] + 2 * P]
                    src = bank[:, :].rearrange("p (h n) -> p h n", h=2)
                else:
                    pos = POS[a[0][2]]
                    dst, src = probs[G % 2][:, head, pos:pos + S], bank[:, :]
                nc.scalar.activation(dst, src, ACT.Exp).then_inc(exp_done, 1)

            def copy_nmax(G):
                ac.wait_ge(nmt_ready, G + 1)
                if G >= 2:
                    ac.wait_ge(nm_rows[G % 2], 64 * (G // 2))
                nc.scalar.activation(nmaxT[:, G % 2, :], MISC[0:GH * PARTS, 0:S // 2].bitcast(bf16), ACT.Copy).then_inc(nmt_sb, 1)

            def copy_out(G):
                ac.wait_ge(pv_ready, G + 1)
                if G >= 1:
                    ac.wait_ge(ott_ready, G)
                nc.scalar.activation(OT[:, :], O_BANK[:, :], ACT.Copy).then_inc(ot_sb, 1)

            def copy_at(b):
                ac.wait_ge(aot_ready, b + 1)
                if b >= 1:
                    ac.wait_ge(wo_ready, b)
                nc.scalar.activation(AT[:, :], M0[:, :], ACT.Copy).then_inc(at_sb, 1)

            PROJECT_ACT = {(2, 5): (split_xt, ln_index(1, 0)), (2, 7): (high_qk, 0, 0), (2, 8): (middle_qk, 0, 0),
                           (3, 0): (high_qk, 0, 1), (3, 1): (middle_qk, 0, 1),
                           (3, 3): (split_xt, ln_index(1, 1)), (3, 4): (high_qk, 1, 0), (3, 5): (middle_qk, 1, 0),
                           (3, 6): (high_qk, 1, 1), (3, 7): (middle_qk, 1, 1)}

            def load_table(k, function):
                nc.scalar.activation(table[:, k:k + 1], rt_raw[:, 0:1], function)

            ac.wait_ge(ld_w[0], 16)
            load_table(0, ACT.Silu)
            for k in range(2):
                high_weights(k)
            split_xt(0)
            for k in range(2, 4):
                high_weights(k)
            router_silu(0)
            ffn(0)
            load_table(1, ACT.Exp)
            for n in STEPS:
                for i in range(NU):
                    if 0 <= n < NGT:
                        exps(n, i)
                    if (n, i) in VALUE_SLOTS:
                        values(VALUE_SLOTS.index((n, i)))
                    if i == 3 and 0 <= n + 1 < NGT:
                        copy_nmax(n + 1)
                    if (b := projected_at(n, 1)) is not None:
                        if i == 9:
                            split_xt(ln_index(1, b))
                    for k in range(2):
                        if (b := projected_at(n, 2 + k)) is not None:
                            if i == (1 if n < 0 else 5):
                                high_qk(b, k)
                            if i == 7:
                                middle_qk(b, k)
                    if (b := batch_at(n, 3)) is not None and i == 9:
                        values(b)
                    if (b := batch_done(n)) is not None and i == 9:
                        copy_at(b)
                    if (n, i) in XT_TAIL:
                        split_xt(ln_index(2, XT_TAIL.index((n, i))))
                    if n == NGT and i == 0:
                        router_silu(B)
                    if n == NGT and i in (1, 5):
                        silu(C * B + i // 4)
                if 0 <= n - 1 < NGT:
                    copy_out(n - 1)
            ffn(1)

        @block.vector
        def _(v):
            count = [0]

            def link(ins):
                count[0] += 1
                ins.then_inc(dve_chain, 1)
                v.wait_ge(dve_chain, count[0])

            def moments(kind, b):
                n = ln_index(kind, b)
                if n >= 1:
                    v.wait_ge(xn_ready, n)
                if kind == 0:
                    v.wait_ge(ld_x[b], 64 if b == 0 else 16)
                elif kind == 1:
                    v.wait_ge(y_used, C * (b + 1))
                else:
                    v.wait_ge(x_att, b + 1)
                for t in range(NT):
                    i = nc.vector.bn_stats(stats[:, t, :], X[:, b * NT + t, :])
                link(i)
                for t in range(NT):
                    i = nc.vector.bn_aggr(mv[:, t, :], stats[:, t, :])
                i.then_inc(mv_ready, 1)

            def split_xt(n):
                v.wait_ge(xh_ready, n + 1)
                nc.vector.tensor_tensor(XL[:, n % 3, :], M0[:, :], XH[:, n % 3, :], ALU.subtract).then_inc(xl_ready, 1)

            halves = M1[:, 0:2 * RW * NT].rearrange("p (t a e) -> p t a e", a=2, e=RW)

            def router_shift(j):
                v.wait_ge(lg_ready, j + 1)
                if j >= 1:
                    v.wait_ge(ex_ready, 2 * j)
                link(nc.vector.tensor_copy(low[:, :, :], halves[:, :, 1, 0:C]))
                link(nc.vector.tensor_tensor(lg[:, :, :], halves[:, :, 0, 0:C], low[:, :, :], ALU.add))
                link(nc.vector.tensor_reduce(nmx[:, :], lg[:, :, 0:E], AX.X, ALU.max, negate=True))
                nc.vector.scalar_tensor_tensor(shifted[:, :, :], lg[:, :, 0:E], -1.0,
                                        nmx[:, :].unsqueeze(2).broadcast_to([P, NT, E]), ALU.add, ALU.add).then_inc(shift_ready, 1)

            def route_exp(j):
                v.wait_ge(ex_ready, 2 * (j + 1))
                if j >= 1:
                    v.wait_ge(coef_ready, j)
                link(nc.vector.tensor_tensor(rest[:, :, :], shifted[:, :, :], sl[:, :, :], ALU.subtract))
                link(nc.vector.reciprocal(rest[:, :, :], rest[:, :, :]))
                link(nc.vector.tensor_tensor(ex[:, :, :], sl[:, :, :], rest[:, :, :], ALU.mult))
                link(nc.vector.tensor_reduce(ssum[:, :], ex[:, :, :], AX.X, ALU.add))
                nc.vector.reciprocal(rsum[:, :], ssum[:, :]).then_inc(sm_ready, 1)

            def route_above(j):
                if j == 0:
                    v.wait_ge(ld_cf, 16)
                v.wait_ge(lead_ready, j + 1)
                nc.vector.tensor_tensor(above[:, :, :, :], lead[:, :, :, :],
                                        least_lead[:, :, :].unsqueeze(1).broadcast_to([P, NT, E, E]),
                                        ALU.is_gt).then_inc(above_ready, 1)

            def gate_up(j):
                i = C * j + E
                v.wait_ge(act_ready, i + 1)
                v.wait_ge(h_ready, HID * (j + 1))
                if j >= 1:
                    v.wait_ge(y_ready, C * j)
                nc.vector.tensor_tensor(gated[:, :], act[:, i % 3, :], H_BANK[(HID * j + E + 1) % 3][:, :],
                                        ALU.mult).then_inc(up_used, 1)

            def accumulate(i):
                j, n = divmod(i, C)
                b = j % B
                v.wait_ge(y_ready, i + 1)
                if n == 0:
                    v.wait_ge(coef_ready, j + 1)
                    if j >= B:
                        v.wait_ge(x_att, b + 1)
                if i >= 1:
                    v.wait_ge(y_used, i)
                for t in range(NT):
                    m = nc.vector.scalar_tensor_tensor(X[:, b * NT + t, :], Y_BANK[i % 3][:, t * P:(t + 1) * P],
                                                       coef[:, j % 2, t, n:n + 1], X[:, b * NT + t, :], ALU.mult, ALU.add)
                m.then_inc(y_used, 1)

            def ffn(kind):
                for b in range(B):
                    j = B * kind + b
                    for n in range(C):
                        if n == C - 2:
                            gate_up(j)
                        accumulate(C * j + n)
                        if b + 1 < B:
                            if n == 0 and j != B:
                                split_xt(ln_index(2 * kind, b + 1))
                            if n == 2:
                                router_shift(j + 1)
                            if n == 3:
                                route_exp(j + 1)
                            if n == 6:
                                route_above(j + 1)
                        if n == 6 and j == B - 3:
                            low_weights(4)
                        if j == B and n == 0:
                            normalise(NGT - 1)
                        if j == B and n == 5:
                            add_attention(B - 1)
                        if (j, n) in PROJECT_DVE:
                            part, *of = PROJECT_DVE[j, n]
                            part(*of)
                        before, after = LATER[kind][b]
                        if before and n == 1:
                            moments(*before)
                        if after and n == (8 if before else 6):
                            moments(*after)

            def rest_qk(b, i):
                v.wait_ge(qk_high, 2 * b + i + 1)
                if b >= 1:
                    v.wait_ge(parts_ready, 2 * (b - 1) + i + 1)
                nc.vector.scalar_tensor_tensor(qk_rest[:, i, :], MISC[:, :], QK_SCALE[i], qk_parts[:, b % 2, i, 0, :],
                                               ALU.mult, ALU.subtract).then_inc(qk_sub, 1)

            def low_weights(k):
                v.wait_ge(w_high, k + 1)
                if k == 0:
                    nc.vector.tensor_tensor(rt_parts[:, RW:2 * RW], rt_raw[:, :], rt_parts[:, 0:RW], ALU.subtract).then_inc(w_split, 1)
                else:
                    c = slice(*CUTS[k - 1])
                    nc.vector.tensor_tensor(w_lo[:, c], w_raw[:, c], w_hi[:, c], ALU.subtract).then_inc(w_split, 1)

            def maxima(G, i):
                u = NU * G + i
                v.wait_ge(s_ready, u + 1)
                if i == 0 and G >= 2:
                    v.wait_ge(nm3_ready, G - 1)
                a = score_units(G % NG)[i]
                bank = S_BANK[u % 3]
                hh = a[0][1] - GH * (G % NG)
                dst = nmax[:, G % 2]
                if a[0][2] == 1:
                    r = nc.vector.tensor_reduce(dst[:, hh:hh + 3:2, 1], bank[:, :].rearrange("p (h n) -> p h n", h=2),
                                                AX.X, ALU.max, negate=True)
                else:
                    for off, _, qt in a:
                        r = nc.vector.tensor_reduce(dst[:, hh, qt:qt + 1], bank[:, off:off + (qt + 1) * P],
                                                    AX.X, ALU.max, negate=True)
                r.then_inc(s_used, 1)

            def normalise(G):
                g = G % NG
                v.wait_ge(ott_ready, G + 1)
                o = MISC[:, :].rearrange("p (t h c) -> p t h c", t=NT, h=GH)
                link(nc.vector.reciprocal(rden[:, :, :], o[:, :, :, HD]))
                if g == 0 and G >= NG:
                    v.wait_ge(aot_ready, G // NG)
                dst = AO[:, :, GH * HD * g:GH * HD * (g + 1)].rearrange("p t (h d) -> p t h d", d=HD)
                i = nc.vector.tensor_tensor(dst, o[:, :, :, 0:HD], rden[:, :, :].unsqueeze(3).broadcast_to([P, NT, GH, HD]),
                                            ALU.mult)
                i.then_inc(ott_used, 1)

            def add_attention(b):
                v.wait_ge(wo_ready, b + 1)
                xt = X[:, b * NT:(b + 1) * NT, :]
                nc.vector.tensor_tensor(xt, xt, M0[:, :].rearrange("p (t d) -> p t d", t=NT), ALU.add).then_inc(x_att, 1)

            PROJECT_DVE = {(2, 4): (split_xt, ln_index(1, 0)), (2, 6): (rest_qk, 0, 0), (2, 8): (rest_qk, 0, 1),
                           (3, 2): (split_xt, ln_index(1, 1)), (3, 3): (rest_qk, 1, 0), (3, 5): (rest_qk, 1, 1)}

            moments(0, 0)
            v.wait_ge(mv_ready, 1)
            rsqrt(nc.vector, link, True)
            for t in range(NT):
                i = nc.vector.tensor_scalar(XN[:, 0, t, :], X[:, t, :], mv[:, t, 0:1], rstd[:, t:t + 1],
                                            ALU.subtract, ALU.mult)
            i.then_inc(xn_ready, 1)
            moments(0, 1)
            low_weights(0)
            split_xt(0)
            low_weights(1)
            low_weights(2)
            router_shift(0)
            low_weights(3)
            route_exp(0)
            route_above(0)
            ffn(0)
            for n in STEPS:
                for i in range(NU):
                    if 0 <= n + 2 < NGT:
                        maxima(n + 2, i)
                    if i == OUT_SLOT and 0 <= n - 2 < NGT:
                        normalise(n - 2)
                    if n == LAST_LN and i == 6:
                        moments(1, B - 1)
                    if (b := projected_at(n, 1)) is not None:
                        if i == 9:
                            split_xt(ln_index(1, b))
                    for k in range(2):
                        if (b := projected_at(n, 2 + k)) is not None and i == (1 if n < 0 else 5):
                            rest_qk(b, k)
                    if (b := batch_done(n - 1)) is not None and i == 1:
                        add_attention(b)
                    if n in (NGT - 6, NGT - 4) and i == 6:
                        moments(2, (n - NGT + 6) // 2)
                    if n == NGT - 1 and i == 1:
                        router_shift(B)
                    if (n, i) in XT_TAIL:
                        split_xt(ln_index(2, XT_TAIL.index((n, i))))
                    if n == NGT and i == 2:
                        route_exp(B)
                    if n == NGT and i == 3:
                        route_above(B)
            ffn(1)

        @block.tensor
        def _(pe):
            def three_pass(dst, w_h, w_l, m_h, m_l):
                nc.tensor.matmul(dst, w_h, m_h, start=True, stop=False)
                nc.tensor.matmul(dst, w_h, m_l, start=False, stop=False)
                return nc.tensor.matmul(dst, w_l, m_h, start=False, stop=True)

            last_use = [None]

            def take_misc(used, value):
                if last_use[0]:
                    pe.wait_ge(*last_use[0])
                last_use[0] = (used, value)

            def transpose_xn(n, used, value):
                pe.wait_ge(xn_ready, n + 1)
                take_misc(used, value)
                for t in range(NT):
                    i = nc.tensor.transpose(M0[:, t * P:(t + 1) * P], XN[:, n % 2, t, :], id_f[:, :])
                i.then_inc(xt_ready, 1)

            def logits(j, n):
                pe.wait_ge(xl_ready, n + 1)
                if j >= 1:
                    pe.wait_ge(shift_ready, j)
                for t in range(NT):
                    c = slice(t * P, (t + 1) * P)
                    dst = M1[:, 2 * RW * t:2 * RW * (t + 1)]
                    nc.tensor.matmul(dst, XH[:, n % 3, c], rt_parts[:, :], start=True, stop=False)
                    i = nc.tensor.matmul(dst, XL[:, n % 3, c], rt_parts[:, :], start=False, stop=True)
                i.then_inc(lg_ready, 1)

            def hidden(j, n):
                i = HID * j + n
                ln = ln_index(2 * (j // B), j % B)
                if n == 0:
                    pe.wait_ge(xl_ready, ln + 1)
                if j == 0 and n in (0, 2, 6):
                    pe.wait_ge(w_split, {0: 2, 2: 3, 6: 4}[n])
                if i >= 3:
                    jj, nn = divmod(i - 3, HID)
                    if nn == E + 1:
                        pe.wait_ge(up_used, jj + 1)
                    else:
                        pe.wait_ge(act_ready, C * jj + nn + 1)
                c = slice(n * F, (n + 1) * F)
                three_pass(H_BANK[i % 3][:, :], w_hi[:, c], w_lo[:, c], XH[:, ln % 3, :], XL[:, ln % 3, :]).then_inc(h_ready, 1)

            def combine(j, n):
                i = C * j + n
                if n == E:
                    pe.wait_ge(up_used, j + 1)
                else:
                    pe.wait_ge(act_ready, i + 1)
                if i >= 3:
                    pe.wait_ge(y_used, i - 2)
                if j == 0 and n == 0:
                    pe.wait_ge(ld_w2, 32)
                if j == B and n == 2:
                    pe.wait_ge(ot_sb, NGT)
                for t in range(NT):
                    r = slice(t * P, (t + 1) * P)
                    a = gated[:, r] if n == E else act[:, i % 3, r]
                    m = nc.tensor.matmul(Y_BANK[i % 3][:, r], a, w2_sb[:, n, :], start=True, stop=True)
                m.then_inc(y_ready, 1)

            def ffn(kind):
                for b in range(B):
                    j, ln = B * kind + b, ln_index(2 * kind, b)
                    if j == 0:
                        hidden(j, 0)
                        hidden(j, 1)
                    for n in range(C):
                        if n + 2 < HID:
                            hidden(j, n + 2)
                        elif b + 1 < B:
                            hidden(j + 1, 0)
                            hidden(j + 1, 1)
                        combine(j, n)
                        if b + 1 < B:
                            if n == 0 and j != B:
                                transpose_xn(ln + 1, xl_ready, ln + 2)
                            if n == 2:
                                logits(j + 1, ln + 1)
                        if (j, n) in PROJECT_PE:
                            if (j, n) == (2, 6):
                                pe.wait_ge(w_split, 5)
                            part, *of = PROJECT_PE[j, n]
                            part(*of)
                        if j == B:
                            if n == 0:
                                transpose_out(NGT - 1)
                            if n == 2:
                                transpose_ao(B - 1)
                            if n == 4:
                                output(B - 1)

            def project(b, i):
                ln = ln_index(1, b)
                pe.wait_ge(xl_ready, ln + 1)
                take_misc(qk_sub, 2 * b + i + 1)
                c = slice((E + 2) * F + i * D, (E + 2) * F + (i + 1) * D)
                three_pass(MISC[:, :], w_hi[:, c], w_lo[:, c], XH[:, ln % 3, :], XL[:, ln % 3, :]).then_inc(qk_ready, 1)

            def values(b):
                ln = ln_index(1, b)
                c = slice((E + 2) * F + 2 * D, (E + 2) * F + 3 * D)
                take_misc(v_sb, b + 1)
                for t in range(NT):
                    r = slice(t * P, (t + 1) * P)
                    m = three_pass(MISC[:, r], XH[:, ln % 3, r], XL[:, ln % 3, r], w_hi[:, c], w_lo[:, c])
                m.then_inc(v_ready, 1)

            def scores(G, i):
                b, g = divmod(G, NG)
                u = NU * G + i
                if u >= 3:
                    pe.wait_ge(s_used, u - 2)
                if i == 0 and g == 0:
                    pe.wait_ge(qa_ready[b % 2], 32 * (b // 2 + 1))
                    pe.wait_ge(ka_ready[b % 2], 32 * (b // 2 + 1))
                for off, h, qt in score_units(g)[i]:
                    lo = 64 * (h % 2)
                    r = slice(lo, lo + ROWS_S)
                    dst = S_BANK[u % 3]
                    n = (qt + 1) * P
                    nc.tensor.matmul(dst[:, off:off + n], QA[b % 2][r, h // 2, qt * P:(qt + 1) * P],
                                     KA[b % 2][r, h // 2, 0:n], start=True, stop=False, skip_group_check=True)
                    m = nc.tensor.matmul(dst[:, off + qt * P:off + n], id_b[:, :], causal_sb[:, :],
                                         start=False, stop=True, skip_group_check=True)
                m.then_inc(s_ready, 1)

            def transpose_nmax(G):
                pe.wait_ge(nm3_ready, G + 1)
                take_misc(nmt_sb, G + 1)
                dst = MISC[0:GH * PARTS, 0:S // 2].bitcast(bf16)
                for t in range(NT):
                    i = nc.tensor.transpose(dst[:, t * P:(t + 1) * P], nmax3[:, t, :, :].rearrange("p h a -> p (h a)"), id_b[:, :])
                i.then_inc(nmt_ready, 1)

            def scores_t(G, i):
                b, g = divmod(G, NG)
                u = NU * G + i
                if i == 0:
                    pe.wait_ge(nm_rows[G % 2], 64 * (G // 2 + 1))
                if u >= 3:
                    pe.wait_ge(exp_done, u - 2)
                for off, h, kt in prob_units(g)[i]:
                    lo = 64 * (h % 2)
                    r = slice(lo, lo + ROWS_T)
                    m = nc.tensor.matmul(T_BANK[u % 3][:, off:off + WID[kt]], KA[b % 2][r, h // 2, kt * P:(kt + 1) * P],
                                         QA[b % 2][r, h // 2, kt * P:S], start=True, stop=True, skip_group_check=True)
                m.then_inc(t_ready, 1)

            PIECES = ((0, 0, 256), (0, 256, 512), (3, 384, 512), (1, 128, 512), (2, 256, 512))
            PIECE_SLOTS = (2, 3, 5, 6, 8)

            def weigh_values(G, k):
                b, g = divmod(G, NG)
                kt, q0, q1 = PIECES[k]
                pe.wait_ge(masked, NT * G + {0: 1, 3: 2, 1: 3, 2: 4}[kt])
                if k == 0:
                    if G >= 1:
                        pe.wait_ge(ot_sb, G)
                    if g == 0:
                        pe.wait_ge(v_sb, b + 1)
                at = POS[kt] - kt * P
                for hh in range(GH):
                    m = nc.tensor.matmul(O_BANK[32 * hh:32 * hh + 32, q0:q1], VA[b % 2][:, kt, GH * g + hh, :],
                                         probs[G % 2][:, hh, at + q0:at + q1],
                                         start=(k == 0), stop=(k == len(PIECES) - 1), skip_group_check=True)
                if k == len(PIECES) - 1:
                    m.then_inc(pv_ready, 1)

            def transpose_out(G):
                pe.wait_ge(ot_sb, G + 1)
                take_misc(ott_used, G + 1)
                for t in range(NT):
                    i = nc.tensor.transpose(MISC[:, t * P:(t + 1) * P], OT[:, t * P:(t + 1) * P], id_f[:, :])
                i.then_inc(ott_ready, 1)

            def transpose_ao(b):
                pe.wait_ge(ott_used, NG * (b + 1))
                take_misc(at_sb, b + 1)
                for t in range(NT):
                    i = nc.tensor.transpose(MISC[:, t * P:(t + 1) * P], AO[:, t, :], id_f[:, :])
                i.then_inc(aot_ready, 1)

            def output(b):
                take_misc(x_att, b + 1)
                for t in range(NT):
                    m = nc.tensor.matmul(MISC[:, t * P:(t + 1) * P], AT[:, t * P:(t + 1) * P], wo_sb[:, :], start=True, stop=True)
                m.then_inc(wo_ready, 1)

            ln0, ln1 = ln_index(1, 0), ln_index(1, 1)
            PROJECT_PE = {(2, 4): (transpose_xn, ln0, xl_ready, ln0 + 1), (2, 6): (project, 0, 0), (2, 8): (project, 0, 1),
                          (3, 2): (transpose_xn, ln1, xl_ready, ln1 + 1), (3, 3): (project, 1, 0), (3, 5): (project, 1, 1)}

            pe.wait_ge(ld_c, 16)
            transpose_xn(0, xl_ready, 1)
            pe.wait_ge(w_split, 1)
            logits(0, 0)
            ffn(0)
            pe.wait_ge(up_used, B)
            pe.wait_ge(ld_ac, 16 * 11)
            for n in STEPS:
                for i in range(NU):
                    if n == 0 and i == 0:
                        pe.wait_ge(y_used, C * B)
                    if 0 <= n < NGT:
                        scores_t(n, i)
                    if 0 <= n + 2 < NGT:
                        scores(n + 2, i)
                    if (n, i) in VALUE_SLOTS:
                        values(VALUE_SLOTS.index((n, i)))
                    if i == 3 and 0 <= n + 1 < NGT:
                        transpose_nmax(n + 1)
                    if i == OUT_SLOT and 0 <= n - 2 < NGT:
                        transpose_out(n - 2)
                    if i in PIECE_SLOTS and 0 <= n - 1 < NGT:
                        weigh_values(n - 1, PIECE_SLOTS.index(i))
                    if (b := projected_at(n, 1)) is not None:
                        if i == 9:
                            transpose_xn(ln_index(1, b), xl_ready, ln_index(1, b) + 1)
                    if (b := projected_at(n, 2)) is not None and i == (0 if n < 0 else 4):
                        project(b, 0)
                    if (b := projected_at(n, 3)) is not None and i == 4:
                        project(b, 1)
                    if (b := batch_at(n, 3)) is not None and i == 9:
                        values(b)
                    if (b := batch_done(n)) is not None and i == 9:
                        transpose_ao(b)
                    if (b := batch_done(n - 1)) is not None and i == 1:
                        output(b)
                    if (n, i) in XT_TAIL:
                        ln = ln_index(2, XT_TAIL.index((n, i)))
                        transpose_xn(ln, xl_ready, ln + 1)
                    if n == NGT - 1 and i == 1:
                        pe.wait_ge(s_used, NU * NGT)
                        logits(B, ln_index(2, 0))
                    if n == NGT and i in (0, 4):
                        pe.wait_ge(exp_done, NU * NGT)
                        hidden(B, i // 4)
            ffn(1)


def kernel(**inputs):
    import numpy as np
    import ml_dtypes
    import concourse.bacc as bacc
    from concourse import mybir
    from concourse.bass_utils import run_bass_kernel_spmd as run

    bf = ml_dtypes.bfloat16
    H, S, E, P = 16, 512, 8, 128
    slopes = np.array([1.0 / ((2.0 ** 8) ** (1.0 / H)) ** (i + 1) for i in range(H)], np.float32)

    def parts(a):
        out, rest = [], np.asarray(a, np.float64)
        for _ in range(3):
            out.append(rest.astype(np.float32).astype(bf))
            rest = rest - out[-1].astype(np.float64)
        return out

    lift = slopes.astype(np.float64)[:, None] * np.arange(S)
    ones = [np.ones((H, S), bf)]
    by_pair = lambda rows: np.ascontiguousarray(np.stack(rows).reshape(len(rows), H // 2, 2, S).transpose(2, 0, 1, 3))
    a = {k: np.asarray(v) for k, v in inputs.items()}
    arrays = {
        "x": a["L0_attn_x"],
        "w1": a["L0_ffn_w1"],
        "w2": a["L0_ffn_w2"],
        "gate_up": a["L0_ffn_shared_gate_up"],
        "down": a["L0_ffn_shared_down"],
        "router": np.concatenate([a["L0_ffn_router_w"], a["L0_ffn_shared_gate_w"], np.zeros((P, 1), np.float32)], 1),
        "wq": a["L0_attn_Wq"].T, "wk": a["L0_attn_Wk"].T, "wv": a["L0_attn_Wv"].T, "wo": a["L0_attn_Wo"].T,
        "q_const": by_pair(ones * 3 + parts(lift)),
        "k_const": by_pair(parts(-lift) + ones * 6),
        "least": np.tril(np.full((E, E), -1.2e-38, np.float32), -1),
        "causal": np.triu(np.full((P, P), -1e30, np.float32), 1).astype(bf),
        "ident": np.eye(P, dtype=np.float32),
        "ident_b": np.eye(P, dtype=np.float32).astype(bf),
    }
    nc = bacc.Bacc("TRN2", target_bir_lowering=False, num_devices=1)
    data, args = {}, []
    for name, v in arrays.items():
        v = np.ascontiguousarray(v)
        data["in_" + name] = v
        args.append(nc.dram_tensor("in_" + name, v.shape, mybir.dt.from_np(v.dtype), kind="ExternalInput").ap())
    args.append(nc.dram_tensor("out_x", a["L0_attn_x"].shape, mybir.dt.float32, kind="ExternalOutput").ap())
    macaron_block(nc, *args)
    r = run(nc, [data], core_ids=[0])
    return r.results[0]["out_x"]
```
